# Optimizing a Trainium2 kernel written in Bass

```python
import numpy as np
import jax
import jax.numpy as jnp

def _softmax(x, axis=-1):
    return jax.nn.softmax(x, axis=axis)

def _gelu(x):
    return jax.nn.gelu(x, approximate=True)

def _silu(x):
    return jax.nn.silu(x)

def _sigmoid(x):
    return jax.nn.sigmoid(x)

def _layernorm(x, axis=-1, eps=1e-05):
    m = jnp.mean(x, axis=axis, keepdims=True)
    v = jnp.var(x, axis=axis, keepdims=True)
    return (x - m) / jnp.sqrt(v + eps)

def _scatter_add(tgt, idx, src, axis=0):
    return tgt.at[idx].add(src)

def _segment_sum(src, seg, n):
    return jax.ops.segment_sum(src, seg, n)
kernel_name = 'mk_seq_preln_d2_jaxref_r4_27be50'

def setup_inputs(seed: int=0):
    np.random.seed(seed)
    _w = jnp.asarray

    def _L0_attn_setup():
        import jax, jax.numpy as jnp
        import numpy as np
        H = 16
        key = jax.random.key(seed)
        ks = jax.random.split(key, 7)
        B, L, D, d = (1, 256, 256, 256 // H)
        s = 0.02
        return {'x': jax.random.normal(ks[0], (B, L, D), jnp.float32), 'Wq': jax.random.normal(ks[1], (D, D), jnp.float32) * s, 'Wk': jax.random.normal(ks[2], (D, D), jnp.float32) * s, 'Wv': jax.random.normal(ks[3], (D, D), jnp.float32) * s, 'Wo': jax.random.normal(ks[4], (D, D), jnp.float32) * s, 'gw': jax.random.normal(ks[5], (1, d), jnp.float32) * s, 'sw': jax.random.normal(ks[6], (1, d), jnp.float32) * s}
    _L0_attn_in = _L0_attn_setup()

    def _L0_ffn_setup():
        import jax, jax.numpy as jnp
        import numpy as np
        N_EMBD = 256
        N_STATE = 1024
        key = jax.random.key(seed)
        k_x, k_w1, k_b1, k_w2, k_b2 = jax.random.split(key, 5)
        x = jax.random.normal(k_x, (4, 512, N_EMBD), dtype=jnp.float32)
        w1 = jax.random.normal(k_w1, (N_EMBD, N_STATE), dtype=jnp.float32) * (1.0 / np.sqrt(N_EMBD))
        b1 = jax.random.normal(k_b1, (N_STATE,), dtype=jnp.float32) * 0.02
        w2 = jax.random.normal(k_w2, (N_STATE, N_EMBD), dtype=jnp.float32) * (1.0 / np.sqrt(N_STATE))
        b2 = jax.random.normal(k_b2, (N_EMBD,), dtype=jnp.float32) * 0.02
        return {'x': x, 'w1': w1, 'b1': b1, 'w2': w2, 'b2': b2}
    _L0_ffn_in = _L0_ffn_setup()

    def _L1_attn_setup():
        import jax, jax.numpy as jnp
        import numpy as np
        H = 4
        GATE_NORM = 16.0
        EPS = 1e-05

        def _gla_forward(x, Wq, Wk, Wv, gk_w1, gk_w2, gk_b2, Wg, g_norm_w, Wo):
            B, T, D = x.shape
            Dk = Wq.shape[1] // H
            Dv = Wv.shape[1] // H
            q = (x @ Wq).reshape(B, T, H, Dk) * Dk ** (-0.5)
            k = (x @ Wk).reshape(B, T, H, Dk)
            v = (x @ Wv).reshape(B, T, H, Dv)
            gk = jax.nn.log_sigmoid(x @ gk_w1 @ gk_w2 + gk_b2) / GATE_NORM
            gk = gk.reshape(B, T, H, Dk)

            def step(S, qkvg):
                qt, kt, vt, gt = qkvg
                S = jnp.exp(gt)[..., None] * S + kt[..., None] * vt[..., None, :]
                ot = jnp.einsum('bhk,bhkv->bhv', qt, S)
                return (S, ot)
            S0 = jnp.zeros((B, H, Dk, Dv), dtype=x.dtype)
            tm = lambda a: jnp.swapaxes(a, 0, 1)
            _, o = jax.lax.scan(step, S0, (tm(q), tm(k), tm(v), tm(gk)))
            o = jnp.swapaxes(o, 0, 1)
            g = (x @ Wg).reshape(B, T, H, Dv)
            o = o * jax.lax.rsqrt(jnp.mean(o * o, axis=-1, keepdims=True) + EPS) * g_norm_w
            o = o * (g * jax.nn.sigmoid(g))
            return o.reshape(B, T, H * Dv) @ Wo
        key = jax.random.key(seed)
        ks = jax.random.split(key, 12)
        B, T, D = (8, 1024, 256)
        Dk_total, Dv_total, Dlow = (D // 2, D, 16)

        def w(k, shape, fan_in):
            return jax.random.normal(k, shape, dtype=jnp.float32) * fan_in ** (-0.5)
        return {'x': jax.random.normal(ks[0], (B, T, D), dtype=jnp.float32), 'Wq': w(ks[1], (D, Dk_total), D), 'Wk': w(ks[2], (D, Dk_total), D), 'Wv': w(ks[3], (D, Dv_total), D), 'gk_w1': w(ks[4], (D, Dlow), D), 'gk_w2': w(ks[5], (Dlow, Dk_total), Dlow), 'gk_b2': jnp.zeros((Dk_total,), dtype=jnp.float32), 'Wg': w(ks[6], (D, Dv_total), D), 'g_norm_w': jnp.ones((Dv_total // H,), dtype=jnp.float32), 'Wo': w(ks[7], (Dv_total, D), Dv_total)}
    _L1_attn_in = _L1_attn_setup()

    def _L1_ffn_setup():
        import jax, jax.numpy as jnp
        import numpy as np
        B, S, H = (2, 1024, 256)
        I = 128
        E = 8
        TOPK = 2
        NGROUP = 2
        TOPK_GROUP = 1
        ROUTED_SCALE = 1.0

        def _silu(x):
            return x * jax.nn.sigmoid(x)
        key = jax.random.key(seed)
        ks = jax.random.split(key, 9)

        def w(k, shape, s=0.05):
            return jax.random.normal(k, shape, dtype=jnp.float32) * s
        return {'hidden_states': jax.random.normal(ks[0], (B, S, H), dtype=jnp.float32), 'router_weight': w(ks[1], (E, H)), 'correction_bias': w(ks[2], (E,)), 'w_gate': w(ks[3], (E, H, I)), 'w_up': w(ks[4], (E, H, I)), 'w_down': w(ks[5], (E, I, H)), 'sw_gate': w(ks[6], (H, I)), 'sw_up': w(ks[7], (H, I)), 'sw_down': w(ks[8], (I, H))}
    _L1_ffn_in = _L1_ffn_setup()
    _d = {'L0_attn_x': _L0_attn_in['x'], 'L0_attn_Wq': _L0_attn_in['Wq'], 'L0_attn_Wk': _L0_attn_in['Wk'], 'L0_attn_Wv': _L0_attn_in['Wv'], 'L0_attn_Wo': _L0_attn_in['Wo'], 'L0_attn_gw': _L0_attn_in['gw'], 'L0_attn_sw': _L0_attn_in['sw'], 'L0_ffn_w1': _L0_ffn_in['w1'], 'L0_ffn_b1': _L0_ffn_in['b1'], 'L0_ffn_w2': _L0_ffn_in['w2'], 'L0_ffn_b2': _L0_ffn_in['b2'], 'L1_attn_Wq': _L1_attn_in['Wq'], 'L1_attn_Wk': _L1_attn_in['Wk'], 'L1_attn_Wv': _L1_attn_in['Wv'], 'L1_attn_gk_w1': _L1_attn_in['gk_w1'], 'L1_attn_gk_w2': _L1_attn_in['gk_w2'], 'L1_attn_gk_b2': _L1_attn_in['gk_b2'], 'L1_attn_Wg': _L1_attn_in['Wg'], 'L1_attn_g_norm_w': _L1_attn_in['g_norm_w'], 'L1_attn_Wo': _L1_attn_in['Wo'], 'L1_ffn_router_weight': _L1_ffn_in['router_weight'], 'L1_ffn_correction_bias': _L1_ffn_in['correction_bias'], 'L1_ffn_w_gate': _L1_ffn_in['w_gate'], 'L1_ffn_w_up': _L1_ffn_in['w_up'], 'L1_ffn_w_down': _L1_ffn_in['w_down'], 'L1_ffn_sw_gate': _L1_ffn_in['sw_gate'], 'L1_ffn_sw_up': _L1_ffn_in['sw_up'], 'L1_ffn_sw_down': _L1_ffn_in['sw_down']}
    _x0 = _d['L0_attn_x']
    _d['L0_attn_x'] = jax.random.normal(jax.random.fold_in(jax.random.key(seed), 1), (2, 2048, 256), dtype=_x0.dtype)
    del _x0
    return _d

def reference(L0_attn_x, L0_attn_Wq, L0_attn_Wk, L0_attn_Wv, L0_attn_Wo, L0_attn_gw, L0_attn_sw, L0_ffn_w1, L0_ffn_b1, L0_ffn_w2, L0_ffn_b2, L1_attn_Wq, L1_attn_Wk, L1_attn_Wv, L1_attn_gk_w1, L1_attn_gk_w2, L1_attn_gk_b2, L1_attn_Wg, L1_attn_g_norm_w, L1_attn_Wo, L1_ffn_router_weight, L1_ffn_correction_bias, L1_ffn_w_gate, L1_ffn_w_up, L1_ffn_w_down, L1_ffn_sw_gate, L1_ffn_sw_up, L1_ffn_sw_down):

    def _L0_attn_ref(x, Wq, Wk, Wv, Wo, gw, sw):
        import jax, jax.numpy as jnp
        import numpy as np
        H = 16
        B, L, D = x.shape
        d = D // H
        Q = (x @ Wq.T).reshape(B, L, H, d)
        K = (x @ Wk.T).reshape(B, L, H, d)
        V = (x @ Wv.T).reshape(B, L, H, d)
        KV = jnp.einsum('blhd,blhe->blhde', K, V)
        g = jax.nn.sigmoid(x.reshape(B, L, H, d) @ gw.T)
        g = jnp.clip(g, 1e-06, None)
        log_c = jnp.clip(jnp.cumsum(jnp.log(g), axis=1), -30.0, 30.0)
        Gc = (jnp.exp(log_c) + 1e-06)[..., None]
        R = jax.nn.silu(K @ sw.T)[..., None]
        S = jnp.cumsum(KV * R / Gc, axis=1) * Gc
        out = jnp.einsum('blhd,blhde->blhe', Q, S).reshape(B, L, D)
        return out @ Wo.T

    def _L0_ffn_ref(x, w1, b1, w2, b2):
        import jax, jax.numpy as jnp
        import numpy as np
        N_EMBD = 256
        N_STATE = 1024
        h = jax.nn.gelu(jnp.einsum('bse,eh->bsh', x, w1) + b1, approximate=False)
        return jnp.einsum('bsh,he->bse', h, w2) + b2

    def _L1_attn_ref(x, Wq, Wk, Wv, gk_w1, gk_w2, gk_b2, Wg, g_norm_w, Wo):
        import jax, jax.numpy as jnp
        import numpy as np
        H = 4
        GATE_NORM = 16.0
        EPS = 1e-05

        def _gla_forward(x, Wq, Wk, Wv, gk_w1, gk_w2, gk_b2, Wg, g_norm_w, Wo):
            B, T, D = x.shape
            Dk = Wq.shape[1] // H
            Dv = Wv.shape[1] // H
            q = (x @ Wq).reshape(B, T, H, Dk) * Dk ** (-0.5)
            k = (x @ Wk).reshape(B, T, H, Dk)
            v = (x @ Wv).reshape(B, T, H, Dv)
            gk = jax.nn.log_sigmoid(x @ gk_w1 @ gk_w2 + gk_b2) / GATE_NORM
            gk = gk.reshape(B, T, H, Dk)

            def step(S, qkvg):
                qt, kt, vt, gt = qkvg
                S = jnp.exp(gt)[..., None] * S + kt[..., None] * vt[..., None, :]
                ot = jnp.einsum('bhk,bhkv->bhv', qt, S)
                return (S, ot)
            S0 = jnp.zeros((B, H, Dk, Dv), dtype=x.dtype)
            tm = lambda a: jnp.swapaxes(a, 0, 1)
            _, o = jax.lax.scan(step, S0, (tm(q), tm(k), tm(v), tm(gk)))
            o = jnp.swapaxes(o, 0, 1)
            g = (x @ Wg).reshape(B, T, H, Dv)
            o = o * jax.lax.rsqrt(jnp.mean(o * o, axis=-1, keepdims=True) + EPS) * g_norm_w
            o = o * (g * jax.nn.sigmoid(g))
            return o.reshape(B, T, H * Dv) @ Wo
        return _gla_forward(x, Wq, Wk, Wv, gk_w1, gk_w2, gk_b2, Wg, g_norm_w, Wo)

    def _L1_ffn_ref(hidden_states, router_weight, correction_bias, w_gate, w_up, w_down, sw_gate, sw_up, sw_down):
        import jax, jax.numpy as jnp
        import numpy as np
        B, S, H = (2, 1024, 256)
        I = 128
        E = 8
        TOPK = 2
        NGROUP = 2
        TOPK_GROUP = 1
        ROUTED_SCALE = 1.0

        def _silu(x):
            return x * jax.nn.sigmoid(x)
        b, s, h = hidden_states.shape
        x = hidden_states.reshape(-1, h)
        logits = x @ router_weight.T
        scores = jax.nn.sigmoid(logits)
        scores_for_choice = scores + correction_bias[None, :]
        e_per_g = E // NGROUP
        group_scores = jax.lax.top_k(scores_for_choice.reshape(-1, NGROUP, e_per_g), 2)[0].sum(-1)
        group_idx = jax.lax.top_k(group_scores, TOPK_GROUP)[1]
        group_mask = jax.nn.one_hot(group_idx, NGROUP, dtype=scores.dtype).sum(1)
        score_mask = jnp.repeat(group_mask, e_per_g, axis=1)
        masked = jnp.where(score_mask > 0, scores_for_choice, 0.0)
        topk_idx = jax.lax.top_k(masked, TOPK)[1]
        topk_w = jnp.take_along_axis(scores, topk_idx, axis=1)
        topk_w = topk_w / (topk_w.sum(-1, keepdims=True) + 1e-20)
        topk_w = topk_w * ROUTED_SCALE
        comb = (jax.nn.one_hot(topk_idx, E, dtype=x.dtype) * topk_w[..., None]).sum(1)
        g = jnp.einsum('th,ehi->tei', x, w_gate)
        u = jnp.einsum('th,ehi->tei', x, w_up)
        y = jnp.einsum('tei,eih->teh', _silu(g) * u, w_down)
        routed = jnp.einsum('teh,te->th', y, comb).reshape(b, s, h)
        shared = _silu(hidden_states @ sw_gate) * (hidden_states @ sw_up) @ sw_down
        return routed + shared
    x = L0_attn_x
    x = x + _L0_attn_ref(_layernorm(x, axis=-1), L0_attn_Wq, L0_attn_Wk, L0_attn_Wv, L0_attn_Wo, L0_attn_gw, L0_attn_sw)
    x = x + _L0_ffn_ref(_layernorm(x, axis=-1), L0_ffn_w1, L0_ffn_b1, L0_ffn_w2, L0_ffn_b2)
    x = x + _L1_attn_ref(_layernorm(x, axis=-1), L1_attn_Wq, L1_attn_Wk, L1_attn_Wv, L1_attn_gk_w1, L1_attn_gk_w2, L1_attn_gk_b2, L1_attn_Wg, L1_attn_g_norm_w, L1_attn_Wo)
    x = x + _L1_ffn_ref(_layernorm(x, axis=-1), L1_ffn_router_weight, L1_ffn_correction_bias, L1_ffn_w_gate, L1_ffn_w_up, L1_ffn_w_down, L1_ffn_sw_gate, L1_ffn_sw_up, L1_ffn_sw_down)
    return x

_drawn_inputs = setup_inputs


def setup_inputs(seed=0):
    import zlib

    import numpy as np

    out = dict(_drawn_inputs(seed))
    spreads = {'L1_attn_gk_b2': (0.0, 0.276), 'L1_attn_g_norm_w': (1.0, 0.2)}
    factors = {'L0_attn_gw': 8.0, 'L0_ffn_b1': 2.862}
    for name, (base, spread) in spreads.items():
        noise = np.random.default_rng([zlib.crc32(name.encode()), seed]).standard_normal(out[name].shape)
        drawn = base * np.exp(spread * noise) if base else spread * noise
        out[name] = jnp.asarray(drawn.astype(out[name].dtype))
    for name, factor in factors.items():
        out[name] = (out[name] * factor).astype(out[name].dtype)
    return out
```

```python
import concourse.bass as bass
from concourse import mybir
from contextlib import ExitStack

P = 128
B, L, D = 2, 2048, 256
UT = 512
NT = UT // P
NU = B * L // UT
KT = D // P
F1 = 1024
NF = F1 // P
H0, D0 = 16, 16
HH = P // D0
H1, DK, DV = 4, 32, 64
NE, IE = 8, 128
EPS = 1e-5
GCLIP = 1e-6
LOG_GCLIP = -13.815510557964274
GATE_NORM = 16.0
SPREAD = 43.0


def layout(parts):
    at, out = 0, {}
    for name, cols in parts:
        out[name] = at
        at += cols
    return out, at


W1, W1_COLS = layout([("k", KT * D), ("gate", P), ("v", KT * D), ("q", KT * D), ("o", KT * D),
                      ("w1", KT * F1), ("w2", NF * D)])
W2, W2_COLS = layout([("router", KT * NE)]
                     + [(f"{n}{e}", KT * IE) for e in range(NE + 1) for n in ("wg", "wu", "wd")])
WG, WG_COLS = layout([("q", KT * 128), ("k", KT * 128), ("vg", KT * 512), ("w1", KT * 16), ("o", KT * D)])
SM, SM_COLS = layout([("swbd", P), ("gkw2", P), ("ident", P), ("causal", P), ("bd16", P), ("bd32", D),
                      ("hm16", HH), ("hm32", H1), ("tri", NE * NE), ("sel", NE), ("b1", NF), ("gkb", 1),
                      ("gnw", DV), ("b2", D), ("cbias", NE)])
PIECE = 1024


def pieces(cols):
    return [(a, min(PIECE, cols - a)) for a in range(0, cols, PIECE)]


def _l0_uses():
    out = ["K0", "Z0", "K1", "Z1", "R0", "V0", "R1", "V1"]
    for hf in range(2):
        out += [f"Q{hf}", f"KT{hf}", f"dS{hf}"] + [f"A{hf}{c}{g}" for c in range(NT) for g in range(2)]
    return out + ["xT0", "xT1", "W0", "W1"]


USES = {
    "l0": _l0_uses(),
    "ffn": ["xT00", "xT01", "xT10", "xT11"] + [f"h{j}" for j in range(NF)],
    "l1": ["low", "vg0", "zg", "vg1", "vg2", "vg3", "q", "k", "A0", "dS0", "A1", "dS1", "A2", "A3", "oT0", "oT1",
           "xT0", "xT1", "W0", "W1"],
    "moe": ["xT0", "xT1", "rt", "cT"] + [f"{n}{e}" for e in range(NE) for n in "guc"] + ["g8", "u8"],
}
RING = {"l0": 2, "l1": 2, "ffn": 3, "moe": 3}
for _s, _u in USES.items():
    assert len(_u) % RING[_s] == 0


def build(nc, x, wm1, wm2, wg, small, scratch, out):
    f32, f32r = mybir.dt.float32, mybir.dt.float32r
    ALU = mybir.AluOpType
    ACT = mybir.ActivationFunctionType
    AX = mybir.AxisListType
    ctx = ExitStack()
    with ctx:
        def sb(name, shape, dt=f32):
            return ctx.enter_context(nc.sbuf_tensor(name, shape, dt))

        sems = {}

        def S(name):
            if name not in sems:
                sems[name] = ctx.enter_context(nc.semaphore(name))
            return sems[name]

        START_AT_ONE = ["free_A0", "free_A1", "free_B0", "free_B1", "free_B2", "accB_free", "ffn_hl", "ffn_dn",
                        "sto0", "sto1"]

        def at(name, n):
            return n + 1 if name in START_AT_ONE else n

        def wait(eng, name, n):
            if not (isinstance(n, int) and n <= 0):
                eng.wait_ge(S(name), at(name, n))

        MCOLS = max(W1_COLS, W2_COLS)
        mh, ml = sb("mh", [P, MCOLS], f32r), sb("ml", [P, MCOLS], f32r)
        gh, gl = sb("gh", [P, WG_COLS], f32r), sb("gl", [P, WG_COLS], f32r)
        sm = sb("sm", [P, SM_COLS])
        selr = sb("selr", [2 * NE, NE], f32r)
        stage = sb("stage", [P, 2, PIECE])
        cst = sb("cst", [P, 16])
        ngkb = sb("ngkb", [P, 1])
        zeros = sb("zeros", [P, 1])
        x0, x1 = sb("x0", [P, 2, NT, D]), sb("x1", [P, 2, NT, D])
        ln = {}
        for t in "ab":
            ln[t] = dict(st=sb(f"st_{t}", [P, NT, 6]), mv=sb(f"mv_{t}", [P, NT, 2]), df=sb(f"df_{t}", [P, NT]), rs=sb(f"rs_{t}", [P, NT]),
                         xn=sb(f"xn_{t}", [P, 2, D]), h=sb(f"xh_{t}", [P, KT, UT], f32r),
                         l=sb(f"xl_{t}", [P, KT, UT], f32r))
        kf, gg = sb("kf", [P, 2, UT]), sb("gg", [P, 2, UT])
        t1, t2, t3 = sb("t1", [P, 2, UT]), sb("t2", [P, 1, UT]), sb("t3", [P, 2, UT])
        qp = sb("qp", [P, UT])
        qx = sb("qx", [P, 2, 4, P])
        VX = 4 * (P + D0)
        vx = sb("vx", [P, 2, VX + 64])
        vtok = sb("vtok", [P, NT, D])
        ktok = sb("ktok", [P, NT, P])
        am = sb("am", [P, 4, UT])
        dst = sb("dst", [P, UT])
        st0 = sb("st0", [P, B, 2, P])
        sx = sb("sx", [P, NT - 1, P])
        cum = sb("cum", [P, B, 2])
        oh, ol = sb("oh", [P, KT, UT], f32r), sb("ol", [P, KT, UT], f32r)
        st1 = sb("st1", [P, B, D])
        sd = sb("sd", [P, NT, D])
        mid = sb("mid", [P, B, NT + 1])
        dec = sb("dec", [P, NT])
        dmid = sb("dmid", [P, NT])
        low = sb("low", [16, UT])
        ss, rr = sb("ss", [P, 2, NT * 2]), sb("rr", [P, 2, NT * 2])
        hfull = sb("hfull", [P, 2, UT])
        hh, hl = sb("hh", [P, 2, UT], f32r), sb("hl", [P, 2, UT], f32r)
        sg = sb("sg", [P, 2, UT])
        sc, sc4 = sb("sc", [P, NT, NE]), sb("sc4", [P, NT, NE])
        pr, gs, gm = sb("pr", [P, NT * 2, 6]), sb("gs", [P, NT, 2]), sb("gm", [P, NT, 2])
        cmp1, cmp2 = sb("cmp1", [P, NT, NE, NE]), sb("cmp2", [P, NT, NE, NE])
        rk, cw = sb("rk", [P, NT, NE]), sb("cw", [P, NT, NE])
        dn = sb("dn", [P, 2, NT])
        cwr = sb("cwr", [P, NT, 2 * NE], f32r)
        cT = sb("cT", [2 * NE, UT], f32r)

        psA = [ctx.enter_context(nc.psum_tensor(f"psA{i}", [P, UT], f32)) for i in range(2)]
        accA = ctx.enter_context(nc.psum_tensor("accA", [P, UT], f32))
        psB = [ctx.enter_context(nc.psum_tensor(f"psB{i}", [P, UT], f32)) for i in range(3)]
        accB = [ctx.enter_context(nc.psum_tensor(f"accB{i}", [P, UT], f32)) for i in range(2)]

        def col(name, n, rows=P):
            return sm[0:rows, SM[name]:SM[name] + n]

        ident, causal = col("ident", P), col("causal", P)

        gate1 = gg[:, :, :].rearrange("p a (b d) -> p (a b) d", d=D)
        on1 = t3[:, :, :].rearrange("p a (b d) -> p (a b) d", d=D)

        class Use:

            def __init__(self, kind, u, name):
                n, i = RING[kind], USES[kind].index(name)
                phase2 = kind in ("l1", "moe")
                before = NU * len(USES["l0" if n == 2 else "ffn"]) // n if phase2 else 0
                self.n = before + u * (len(USES[kind]) // n) + i // n
                if n == 2:
                    if name[0] == "x":
                        self.n = before if isinstance(u, int) and u == 0 \
                            else before + 1 + (u - 1) * (len(USES[kind]) // n) + i // n
                    elif not (isinstance(u, int) and u == NU - 1 and name[0] == "W"):
                        self.n = self.n + 1
                self.ps = (psA if n == 2 else psB)[i % n]
                ring = "A" if n == 2 else "B"
                self.full, self.free = f"full_{ring}{i % n}", f"free_{ring}{i % n}"

            def claim(self, eng):
                wait(eng, self.free, self.n)

            def filled(self, eng):
                eng.wait_ge(S(self.full), self.n + 1)

            def emptied(self, eng):
                eng.wait_ge(S(self.free), at(self.free, self.n + 1))

        STREAM = {"l0": "a", "l1": "a", "ffn": "b", "moe": "b"}
        LAST_XT = {"l0": "Q1", "ffn": f"h{NF - 1}", "l1": "k", "moe": "u8"}

        def seq(kind, u):
            return (NU if kind in ("l1", "moe") else 0) + u

        def xt_unused(eng, kind, u):
            if kind == "ffn":
                wait(eng, "ffn_dn", u * NF)
            elif isinstance(u, int) and u == 0:
                if kind in ("l1", "moe"):
                    k = "l0" if kind == "l1" else "ffn"
                    Use(k, NU - 1, LAST_XT[k]).filled(eng)
            else:
                Use(kind, u - 1, LAST_XT[kind]).filled(eng)

        def bc(ap, axis, shape):
            return ap.unsqueeze(axis).to_broadcast(shape)

        def flat(ap):
            return ap.rearrange("p a b -> p (a b)")

        def mm3(pe, psum, wh, wl, xh, xl, first, last):
            pe.matmul(psum, wh, xh, start=first, stop=False, skip_group_check=True)
            pe.matmul(psum, wh, xl, start=False, stop=False, skip_group_check=True)
            return pe.matmul(psum, wl, xh, start=False, stop=last, skip_group_check=True)

        def proj(pe, psum, t, wh, wl, at, stride, m):
            for k in range(KT):
                c = at + k * stride
                last = mm3(pe, psum, wh[:, c:c + m], wl[:, c:c + m], ln[t]["h"][:, k, :], ln[t]["l"][:, k, :],
                           k == 0, k == KT - 1)
            return last

        def ln_dve(dve, kind, u, xsrc):
            t, n = STREAM[kind], seq(kind, u)
            d = ln[t]
            for j in range(NT):
                dve.bn_stats(d["st"][:, j, :], xsrc[:, j, :]).then_inc(S(f"bn_{t}"), 1)
            st, mv, df = d["st"], d["mv"], d["df"]
            dve.wait_ge(S(f"bn_{t}"), n * NT + NT)
            dve.tensor_tensor(df[:, :], st[:, :, 1], st[:, :, 4], ALU.subtract).then_inc(S(f"df_{t}"), 1)
            dve.tensor_tensor(mv[:, :, 0], st[:, :, 1], st[:, :, 4], ALU.add).then_inc(S(f"sm_{t}"), 1)
            dve.tensor_tensor(mv[:, :, 1], st[:, :, 2], st[:, :, 5], ALU.add).then_inc(S(f"m2_{t}"), 1)
            dve.wait_ge(S(f"df_{t}"), n * 2 + 1)
            dve.tensor_tensor(df[:, :], df[:, :], df[:, :], ALU.mult).then_inc(S(f"df_{t}"), 1)
            dve.wait_ge(S(f"sm_{t}"), n * 2 + 1)
            dve.tensor_scalar(mv[:, :, 0], mv[:, :, 0], 0.5, None, ALU.mult).then_inc(S(f"sm_{t}"), 1)
            dve.wait_ge(S(f"m2_{t}"), n + 1)
            dve.wait_ge(S(f"df_{t}"), n * 2 + 2)
            dve.scalar_tensor_tensor(out=mv[:, :, 1], in0=df[:, :], scalar=D / 4.0, in1=mv[:, :, 1], op0=ALU.mult,
                                     op1=ALU.add).then_inc(S(f"mv_{t}"), 1)

        def norm_dve(dve, kind, u, xsrc):
            t, n = STREAM[kind], seq(kind, u)
            d = ln[t]
            dve.wait_ge(S(f"sm_{t}"), n * 2 + 2)
            dve.wait_ge(S(f"rs_{t}"), n + 1)
            for j in range(NT):
                if j >= 2:
                    if kind == "ffn":
                        Use(kind, u, "xT01").filled(dve)
                    else:
                        dve.wait_ge(S(f"tp_{kind}"), u * 2 + j - 1)
                dve.tensor_scalar(d["xn"][:, j % 2, :], xsrc[:, j, :], d["mv"][:, j, 0:1], d["rs"][:, j:j + 1],
                                  ALU.subtract, ALU.mult).then_inc(S(f"xn_{t}"), 1)

        def ln_act(act, kind, u):
            t, n = STREAM[kind], seq(kind, u)
            d = ln[t]
            act.wait_ge(S(f"mv_{t}"), n + 1)
            act.activation(d["rs"][:, :], d["mv"][:, :, 1], ACT.Ln, bias=cst[:, 0:1], scale=1.0 / D).then_inc(S(f"lv_{t}"), 1)
            act.wait_ge(S(f"lv_{t}"), n + 1)
            act.activation(d["rs"][:, :], d["rs"][:, :], ACT.Exp, scale=-0.5).then_inc(S(f"rs_{t}"), 1)

        def xt_names(kind):
            if kind == "ffn":
                return [(f"xT{h}{f}", f, 2 * h, 2) for h in range(2) for f in range(KT)]
            return [(f"xT{f}", f, 0, NT) for f in range(KT)]

        def xt_pe(pe, kind, u):
            t, n = STREAM[kind], seq(kind, u)
            for j in range(NT):
                for name, f, j0, nj in xt_names(kind):
                    if not j0 <= j < j0 + nj:
                        continue
                    use = Use(kind, u, name)
                    if j == j0:
                        use.claim(pe)
                    if f == 0:
                        pe.wait_ge(S(f"xn_{t}"), n * NT + j + 1)
                    last = pe.transpose(use.ps[:, (j - j0) * P:(j - j0 + 1) * P],
                                        ln[t]["xn"][:, j % 2, f * P:(f + 1) * P], ident)
                    if j == j0 + nj - 1:
                        last.then_inc(S(use.full), 1)
                    elif f == KT - 1 and kind != "ffn" and j < 2:
                        last.then_inc(S(f"tp_{kind}"), 1)

        def xt_act(act, kind, u):
            t = STREAM[kind]
            xt_unused(act, kind, u)
            for name, f, j0, nj in xt_names(kind):
                use = Use(kind, u, name)
                use.filled(act)
                act.activation(ln[t]["h"][:, f, j0 * P:(j0 + nj) * P], use.ps[:, 0:nj * P], ACT.Copy)\
                   .then_inc(S(f"xh_{kind}"), 1)

        def xt_dve(dve, kind, u):
            t = STREAM[kind]
            names = xt_names(kind)
            for i, (name, f, j0, nj) in enumerate(names):
                use = Use(kind, u, name)
                dve.wait_ge(S(f"xh_{kind}"), u * len(names) + i + 1)
                dve.tensor_tensor(ln[t]["l"][:, f, j0 * P:(j0 + nj) * P], use.ps[:, 0:nj * P],
                                  ln[t]["h"][:, f, j0 * P:(j0 + nj) * P], ALU.subtract).then_inc(S(use.free), 1)

        def xt_ready(pe, kind, u):
            for name, *_ in xt_names(kind):
                Use(kind, u, name).emptied(pe)

        def wo_pe(pe, kind, u, wh, wl, at):
            for i in range(2):
                use = Use(kind, u, f"W{i}")
                use.claim(pe)
                for jj in range(2):
                    j = 2 * i + jj
                    for k in range(KT):
                        last = mm3(pe, use.ps[:, jj * D:(jj + 1) * D], oh[:, k, j * P:(j + 1) * P],
                                   ol[:, k, j * P:(j + 1) * P], wh[:, at + k * D:at + (k + 1) * D],
                                   wl[:, at + k * D:at + (k + 1) * D], jj == 0 and k == 0, jj == 1 and k == KT - 1)
                last.then_inc(S(use.full), 1)

        def wo_dve(dve, kind, U):
            u, p, q = U
            wait(dve, f"sto{p}", 16 * (q + (NU // 2 if kind == "l1" else 0)))
            for i in range(2):
                use = Use(kind, u, f"W{i}")
                use.filled(dve)
                dve.tensor_tensor(flat(x1[:, p, 2 * i:2 * i + 2, :]), flat(x0[:, p, 2 * i:2 * i + 2, :]),
                                  use.ps[:, :], ALU.add).then_inc(S(use.free), 1)

        def x1_ready(eng, kind, u):
            for i in range(2):
                Use(kind, u, f"W{i}").emptied(eng)

        def n0(u, hf, c, g):
            return u * 16 + hf * 8 + c * 2 + g

        def l0_pe(pe, U, s):
            u, p, q = U
            if s == 1:
                xt_pe(pe, "l0", u)
            elif s in (2, 3):
                hf = s - 2
                if s == 2:
                    xt_ready(pe, "l0", u)
                    if isinstance(u, int) and u == 0:
                        pe.wait_ge(S("w_lo"), L0_PIECES)
                use = Use("l0", u, f"K{hf}")
                use.claim(pe)
                proj(pe, use.ps[:, :], "a", mh, ml, W1["k"] + hf * P, D, P).then_inc(S(use.full), 1)
                use = Use("l0", u, f"Z{hf}")
                use.claim(pe)
                c = W1["gate"]
                mm3(pe, use.ps[:, :], mh[:, c:c + P], ml[:, c:c + P], ln["a"]["h"][:, hf, :],
                    ln["a"]["l"][:, hf, :], True, True).then_inc(S(use.full), 1)
            elif s in (4, 5):
                hf = s - 4
                use = Use("l0", u, f"R{hf}")
                use.claim(pe)
                Use("l0", u, f"K{hf}").emptied(pe)
                pe.matmul(use.ps[:, :], col("swbd", P), kf[:, hf, :], start=True, stop=True)\
                  .then_inc(S(use.full), 1)
                use = Use("l0", u, f"V{hf}")
                use.claim(pe)
                for i in range(2):
                    j = 2 * hf + i
                    for k in range(KT):
                        c = W1["v"] + k * D
                        last = mm3(pe, use.ps[:, i * D:(i + 1) * D], ln["a"]["h"][:, k, j * P:(j + 1) * P],
                                   ln["a"]["l"][:, k, j * P:(j + 1) * P], mh[:, c:c + D], ml[:, c:c + D],
                                   i == 0 and k == 0, i == 1 and k == KT - 1)
                last.then_inc(S(use.full), 1)
            elif s in (6, 12):
                hf = (s - 6) // 6
                use = Use("l0", u, f"Q{hf}")
                use.claim(pe)
                proj(pe, use.ps[:, :], "a", mh, ml, W1["q"] + hf * P, D, P).then_inc(S(use.full), 1)
                if hf == 1:
                    l0_out(pe, U, 0, NT - 1)
            elif s in (7, 13):
                hf = (s - 7) // 6
                use = Use("l0", u, f"KT{hf}")
                use.claim(pe)
                pe.wait_ge(S("l0_kw"), u * 2 + hf + 1)
                for c in range(NT):
                    last = pe.transpose(use.ps[:, c * P:(c + 1) * P], kf[:, hf, c * P:(c + 1) * P], ident)
                last.then_inc(S(use.full), 1)
            elif s in (8, 14):
                hf = (s - 8) // 6
                use = Use("l0", u, f"dS{hf}")
                use.claim(pe)
                Use("l0", u, f"KT{hf}").emptied(pe)
                for c in range(NT):
                    last = pe.matmul(use.ps[:, c * P:(c + 1) * P], ktok[:, c, :], vtok[:, c, hf * P:(hf + 1) * P],
                                     start=c == 0, stop=c == NT - 1, skip_group_check=True)
                last.then_inc(S(use.full), 1)
                l0_scores(pe, U, hf, 0)
            elif s in (9, 10, 11, 15, 16, 17):
                hf, c = (s - 9) // 6, (s - 9) % 6 + 1
                l0_scores(pe, U, hf, c)
                l0_out(pe, U, hf, c - 1)
            elif s == 18:
                l0_out(pe, U, 1, NT - 1)
            elif s == 19:
                pe.wait_ge(S("l0_ol"), u * 2 + 2)
                wo_pe(pe, "l0", u, mh, ml, W1["o"])

        def l0_scores(pe, U, hf, c):
            u = U[0]
            for g in range(2):
                use = Use("l0", u, f"A{hf}{c}{g}")
                use.claim(pe)
                pe.wait_ge(S("l0_qx"), n0(u, hf, c, g) + 1)
                pe.matmul(use.ps[:, :], kf[:, hf, c * P:(c + 1) * P], flat(qx[:, g, :, :]), start=True,
                          stop=True).then_inc(S(use.full), 1)

        def l0_out(pe, U, hf, c):
            u, p, q = U
            o = accA[:, c * P:(c + 1) * P]
            if c == 0:
                wait(pe, "l0_ol", u * 2 + hf)
                state = st0[:, p, hf, :]
            else:
                pe.wait_ge(S("l0_sx"), u * 6 + hf * 3 + c)
                state = sx[:, c - 1, :]
            pe.matmul(o, state, qp[:, c * P:(c + 1) * P], start=c == 0, stop=False,
                      skip_group_check=True).then_inc(S("l0_inter"), 1)
            for g in range(2):
                m = n0(u, hf, c, g)
                pe.wait_ge(S("l0_vx"), m + 1)
                Use("l0", u, f"A{hf}{c}{g}").emptied(pe)
                for h in range(4):
                    last = pe.matmul(o, vx[:, g, h * P:(h + 1) * P], am[:, (2 * c + g) % 4, h * P:(h + 1) * P],
                                     start=False, stop=c == NT - 1 and g == 1 and h == 3, skip_group_check=True)
                last.then_inc(S("l0_av"), 1)

        def l0_act(act, U, s):
            u, p, q = U
            if s == 0:
                if not (isinstance(u, int) and u <= 1):
                    act.preload_act_table_set("natural_log_exp_and_others")
                ln_act(act, "l0", u)
            elif s == 1:
                xt_act(act, "l0", u)
            elif s in (2, 3):
                hf = s - 2
                m = u * 2 + hf + 1
                use = Use("l0", u, f"K{hf}")
                use.filled(act)
                act.activation(kf[:, hf, :], use.ps[:, :], ACT.Copy).then_inc(S(use.free), 1)
                Use("l0", u, f"Z{hf}").emptied(act)
                act.activation(t1[:, hf, :], t1[:, hf, :], ACT.Exp, scale=-1.0).then_inc(S("l0_ez"), 1)
                act.wait_ge(S("l0_ez"), m)
                act.activation(t1[:, hf, :], t1[:, hf, :], ACT.Ln, bias=1.0).then_inc(S("l0_nlg"), 1)
            elif s in (4, 5):
                hf = s - 4
                m = u * 2 + hf + 1
                use = Use("l0", u, f"R{hf}")
                use.filled(act)
                act.activation(t3[:, hf, :], use.ps[:, :], ACT.Exp, scale=-1.0).then_inc(S("l0_er"), 1)
                use = Use("l0", u, f"V{hf}")
                use.filled(act)
                act.activation(flat(vtok[:, 2 * hf:2 * hf + 2, :]), use.ps[:, :], ACT.Copy)\
                   .then_inc(S(use.free), 1)
                act.wait_ge(S("l0_er"), m)
                act.activation(t3[:, hf, :], t3[:, hf, :], ACT.Ln, bias=1.0).then_inc(S("l0_lr"), 1)
                act.wait_ge(S("l0_clip"), m)
                act.activation(gg[:, hf, :], t1[:, hf, :], ACT.Exp, scale=-1.0).then_inc(S("l0_gc"), 1)
                act.wait_ge(S("l0_gc"), m)
                act.activation(t1[:, hf, :], gg[:, hf, :], ACT.Ln, bias=cst[:, 1:2]).then_inc(S("l0_lg"), 1)
            elif s == 6:
                for hf in range(2):
                    act.wait_ge(S("l0_sum"), u * 2 + hf + 1)
                    act.activation(t3[:, hf, :], t3[:, hf, :], ACT.Exp, scale=-1.0).then_inc(S("l0_ew"), 1)
            elif s in (13, 18):
                hf = 0 if s == 13 else 1
                act.wait_ge(S("l0_av"), n0(u, hf, NT - 1, 1) + 1)
                if not (isinstance(u, int) and u == 0):
                    Use("l0", u - 1, "W1").filled(act)
                act.activation(oh[:, hf, :], accA[:, :], ACT.Copy).then_inc(S("l0_oh"), 1)

        def l0_dve(dve, U, s):
            u, p, q = U
            if s == 0:
                dve.wait_ge(S(f"ld{p}"), 16 * (q + 1))
                ln_dve(dve, "l0", u, x0[:, p])
            elif s == 1:
                norm_dve(dve, "l0", u, x0[:, p])
                xt_dve(dve, "l0", u)
            elif s in (2, 3):
                hf = s - 2
                use = Use("l0", u, f"Z{hf}")
                use.filled(dve)
                dve.tensor_scalar(t1[:, hf, :], use.ps[:, :], LOG_GCLIP, None, ALU.max).then_inc(S(use.free), 1)
            elif s in (4, 5):
                hf = s - 4
                m = u * 2 + hf + 1
                dve.wait_ge(S("l0_nlg"), m)
                dve.tensor_tensor_scan(t1[:, hf, :], t1[:, hf, :], zeros[:, 0:1].to_broadcast([P, UT]),
                                       cum[:, p, hf:hf + 1], ALU.add, ALU.add).then_inc(S("l0_cum"), 1)
                use = Use("l0", u, f"R{hf}")
                use.filled(dve)
                dve.wait_ge(S("l0_er"), m)
                dve.tensor_tensor(kf[:, hf, :], kf[:, hf, :], use.ps[:, :], ALU.mult).then_inc(S(use.free), 1)
                dve.wait_ge(S("l0_cum"), m)
                dve.tensor_copy(cum[:, p, hf:hf + 1], t1[:, hf, UT - 1:UT]).then_inc(S("l0_car"), 1)
                dve.wait_ge(S("l0_car"), m)
                dve.tensor_scalar(t1[:, hf, :], t1[:, hf, :], 30.0, -30.0, ALU.min, ALU.max)\
                   .then_inc(S("l0_clip"), 1)
            elif s in (6, 12):
                hf = (s - 6) // 6
                m = u * 2 + hf + 1
                if hf == 0:
                    for h in range(2):
                        dve.wait_ge(S("l0_lg"), m + h)
                        dve.tensor_tensor(t3[:, h, :], t3[:, h, :], t1[:, h, :], ALU.add).then_inc(S("l0_sum"), 1)
                    for h in range(2):
                        dve.wait_ge(S("l0_ew"), m + h)
                        dve.tensor_tensor(kf[:, h, :], kf[:, h, :], t3[:, h, :], ALU.mult).then_inc(S("l0_kw"), 1)
                use = Use("l0", u, f"Q{hf}")
                use.filled(dve)
                wait(dve, "l0_inter", u * 8 + hf * 4)
                dve.wait_ge(S("l0_gc"), m)
                dve.scalar_tensor_tensor(out=qp[:, :], in0=gg[:, hf, :], scalar=GCLIP, in1=use.ps[:, :],
                                         op0=ALU.add, op1=ALU.mult).then_inc(S(use.free), 1)
            elif s in (7, 13):
                hf = (s - 7) // 6
                use = Use("l0", u, f"KT{hf}")
                use.filled(dve)
                dve.tensor_copy(flat(ktok[:, :, :]), use.ps[:, :]).then_inc(S(use.free), 1)
                if hf == 1:
                    l0_low(dve, U, 0)
            elif s in (8, 14):
                hf = (s - 8) // 6
                m = u * 6 + hf * 3
                use = Use("l0", u, f"dS{hf}")
                use.filled(dve)
                wait(dve, "l0_inter", u * 8 + hf * 4)
                dve.tensor_tensor(dst[:, :].rearrange("p (c e) -> p c e", c=NT),
                                  use.ps[:, :].rearrange("p (c e) -> p c e", c=NT),
                                  bc(col("bd16", P), 1, [P, NT, P]), ALU.mult).then_inc(S(use.free), 1)
                use.emptied(dve)
                dve.tensor_tensor(sx[:, 0, :], st0[:, p, hf, :], dst[:, 0:P], ALU.add).then_inc(S("l0_sx"), 1)
                for c in range(1, NT - 1):
                    dve.wait_ge(S("l0_sx"), m + c)
                    dve.tensor_tensor(sx[:, c, :], sx[:, c - 1, :], dst[:, c * P:(c + 1) * P], ALU.add)\
                       .then_inc(S("l0_sx"), 1)
                l0_mask(dve, U, hf, 0)
            elif s in (9, 10, 11, 15, 16, 17):
                hf, c = (s - 9) // 6, (s - 9) % 6 + 1
                l0_mask(dve, U, hf, c)
                if c == 2:
                    dve.wait_ge(S("l0_inter"), u * 8 + hf * 4 + 1)
                    dve.wait_ge(S("l0_sx"), u * 6 + hf * 3 + 3)
                    dve.tensor_tensor(st0[:, p, hf, :], sx[:, NT - 2, :], dst[:, (NT - 1) * P:NT * P], ALU.add)\
                       .then_inc(S("l0_st"), 1)
            elif s == 18:
                l0_low(dve, U, 1)
            elif s == 19:
                wo_dve(dve, "l0", U)

        def l0_mask(dve, U, hf, c):
            u = U[0]
            for g in range(2):
                use = Use("l0", u, f"A{hf}{c}{g}")
                use.filled(dve)
                wait(dve, "l0_av", n0(u, hf, c, g) - 3)
                dve.tensor_tensor(am[:, (2 * c + g) % 4, :].rearrange("p (h t) -> p h t", h=4),
                                  use.ps[:, :].rearrange("p (h t) -> p h t", h=4),
                                  bc(causal, 1, [P, 4, P]), ALU.mult).then_inc(S(use.free), 1)

        def l0_low(dve, U, hf):
            dve.wait_ge(S("l0_oh"), U[0] * 2 + hf + 1)
            dve.tensor_tensor(ol[:, hf, :], accA[:, :], oh[:, hf, :], ALU.subtract).then_inc(S("l0_ol"), 1)

        def l0_pool(pool, U, s):
            u, p, q = U
            if s not in (7, 8, 9, 10, 13, 14, 15, 16):
                return
            hf, c = (s - 7) // 6, (s - 7) % 6
            for g in range(2):
                m = n0(u, hf, c, g)
                Use("l0", u, f"Q{hf}").emptied(pool)
                if c == 0:
                    if not (isinstance(u, int) and u == 0 and hf == 0):
                        Use("l0", u - 1 if hf == 0 else u, f"A{1 - hf}{NT - 1}{g}").filled(pool)
                else:
                    Use("l0", u, f"A{hf}{c - 1}{g}").filled(pool)
                h0 = 4 * g
                pool.tensor_tensor(qx[:, g, :, :], bc(qp[:, c * P:(c + 1) * P], 1, [P, 4, P]),
                                   bc(col("hm16", HH)[:, h0:h0 + 4], 2, [P, 4, P]), ALU.mult)\
                    .then_inc(S("l0_qx"), 1)
            for g in range(2):
                m = n0(u, hf, c, g)
                Use("l0", u, f"V{c // 2}").emptied(pool)
                wait(pool, "l0_av", m - 1)
                d = vx[:, g, g * 64:g * 64 + VX].rearrange("p (h x) -> p h x", x=P + D0)[:, :, 0:D0]
                at = hf * P + g * 64
                v = vtok[:, c, at:at + 64].rearrange("p (h e) -> p h e", e=D0)
                pool.tensor_tensor(d, v, bc(zeros[:, 0:1], 2, [P, 4, D0]), ALU.add).then_inc(S("l0_vx"), 1)

        def ffn_pe(pe, U, s):
            u, p, q = U
            if s == 1:
                xt_pe(pe, "ffn", u)
            elif s >= 2:
                j = s - 2
                if j == 0:
                    xt_ready(pe, "ffn", u)
                    if isinstance(u, int) and u == 0:
                        pe.wait_ge(S("w_lo"), M1_PIECES)
                if j < NF:
                    use = Use("ffn", u, f"h{j}")
                    use.claim(pe)
                    proj(pe, use.ps[:, :], "b", mh, ml, W1["w1"] + j * P, F1, P).then_inc(S(use.full), 1)
                if j >= 2:
                    i = j - 2
                    pe.wait_ge(S("ffn_hl"), at("ffn_hl", u * NF + i + 1))
                    down_pe(pe, "ffn", u, i, NF, W1["w2"] + i * D, "ffn_dn")

        def down_pe(pe, kind, u, i, n, at, done):
            if i == 0:
                wait(pe, "accB_free", seq(kind, u) * 2)
            for j in range(NT):
                last = mm3(pe, accB[j // 2][:, (j % 2) * D:(j % 2 + 1) * D], hh[:, i % 2, j * P:(j + 1) * P],
                           hl[:, i % 2, j * P:(j + 1) * P], mh[:, at:at + D], ml[:, at:at + D],
                           i == 0 and j % 2 == 0, i == n - 1 and j % 2 == 1)
            last.then_inc(S(done), 1)

        def ffn_act(act, U, s):
            u, p, q = U
            if s == 0:
                ln_act(act, "ffn", u)
            elif s == 1:
                xt_act(act, "ffn", u)
            elif s - 2 < NF:
                j = s - 2
                use = Use("ffn", u, f"h{j}")
                use.filled(act)
                wait(act, "ffn_hl", u * NF + max(j - 1, 0))
                act.activation(hfull[:, j % 2, :], use.ps[:, :], ACT.Gelu, bias=col("b1", NF)[:, j:j + 1])\
                   .then_inc(S(use.free), 1)

        def ffn_dve(dve, U, s):
            u, p, q = U
            if s == 0:
                x1_ready(dve, "l0", u)
                ln_dve(dve, "ffn", u, x1[:, p])
            elif s == 1:
                norm_dve(dve, "ffn", u, x1[:, p])
                xt_dve(dve, "ffn", u)
            elif s - 2 < NF:
                j = s - 2
                Use("ffn", u, f"h{j}").emptied(dve)
                wait(dve, "ffn_dn", u * NF + max(j - 1, 0))
                dve.tensor_copy(hh[:, j % 2, :], hfull[:, j % 2, :]).then_inc(S("ffn_hh"), 1)
                dve.wait_ge(S("ffn_hh"), u * NF + j + 1)
                dve.tensor_tensor(hl[:, j % 2, :], hfull[:, j % 2, :], hh[:, j % 2, :], ALU.subtract)\
                   .then_inc(S("ffn_hl"), 1)
            elif s == 11:
                dve.wait_ge(S("ffn_xb"), u + 1)
                dve.wait_ge(S("ffn_dn"), at("ffn_dn", u * NF + NF))
                resid_dve(dve, U)

        def resid_dve(dve, U):
            p = U[1]
            for i in range(2):
                x = flat(x1[:, p, 2 * i:2 * i + 2, :])
                dve.tensor_tensor(x, x, accB[i][:, :], ALU.add).then_inc(S("accB_free"), 1)

        def ffn_pool(pool, U, s):
            u, p, q = U
            if s == 1:
                pool.wait_ge(S("xn_b"), seq("ffn", u) * NT + NT)
                pool.tensor_tensor(x1[:, p, :, :], x1[:, p, :, :], bc(col("b2", D), 1, [P, NT, D]), ALU.add)\
                    .then_inc(S("ffn_xb"), 1)

        def l1_pe(pe, U, s):
            u, p, q = U
            if s == 1:
                xt_pe(pe, "l1", u)
            elif s == 2:
                xt_ready(pe, "l1", u)
                if isinstance(u, int) and u == 0:
                    pe.wait_ge(S("w_lo"), M1_PIECES + G_PIECES)
                use = Use("l1", u, "low")
                use.claim(pe)
                proj(pe, use.ps[0:16, :], "a", gh, gl, WG["w1"], 16, 16).then_inc(S(use.full), 1)
                l1_vg(pe, U, 0)
            elif s == 3:
                use = Use("l1", u, "zg")
                use.claim(pe)
                Use("l1", u, "low").emptied(pe)
                pe.matmul(use.ps[:, :], col("gkw2", P, 16), low[:, :], start=True, stop=True)\
                  .then_inc(S(use.full), 1)
                l1_vg(pe, U, 1)
            elif s in (4, 5):
                l1_vg(pe, U, s - 2)
            elif s == 6:
                for name in "qk":
                    use = Use("l1", u, name)
                    use.claim(pe)
                    proj(pe, use.ps[:, :], "a", gh, gl, WG[name], P, P).then_inc(S(use.full), 1)
            elif s == 7:
                wait(pe, "l1_acc", u * 3)
                Use("l1", u, "k").emptied(pe)
                for c in range(NT):
                    last = pe.transpose(accA[:, c * P:(c + 1) * P], kf[:, 0, c * P:(c + 1) * P], ident)
                last.then_inc(S("l1_kt"), 1)
            elif 8 <= s <= 12:
                c = s - 8
                if c in (1, 2):
                    use = Use("l1", u, f"dS{c - 1}")
                    use.claim(pe)
                    pe.wait_ge(S("l1_acc"), u * 3 + 1)
                    if c == 2:
                        Use("l1", u, "vg2").emptied(pe)
                    for i in range(2):
                        cc = 2 * (c - 1) + i
                        last = pe.matmul(use.ps[:, i * D:(i + 1) * D], ktok[:, cc, :], vtok[:, cc, :],
                                         start=i == 0, stop=i == 1, skip_group_check=True)
                    last.then_inc(S(use.full), 1)
                if c < NT:
                    use = Use("l1", u, f"A{c}")
                    use.claim(pe)
                    pe.wait_ge(S("l1_qx"), u * NT + c + 1)
                    pe.matmul(use.ps[:, :], kf[:, 0, c * P:(c + 1) * P], flat(qx[:, c % 2, :, :]), start=True,
                              stop=True).then_inc(S(use.full), 1)
                if c >= 1:
                    l1_out(pe, U, c - 1)
            elif s == 13:
                for f in range(KT):
                    use = Use("l1", u, f"oT{f}")
                    use.claim(pe)
                    pe.wait_ge(S("l1_on"), u * 2 + 2)
                    for c in range(NT):
                        last = pe.transpose(use.ps[:, c * P:(c + 1) * P], on1[:, c, f * P:(f + 1) * P], ident)
                    last.then_inc(S(use.full), 1)
            elif s == 14:
                for f in range(KT):
                    Use("l1", u, f"oT{f}").emptied(pe)
                wo_pe(pe, "l1", u, gh, gl, WG["o"])

        def l1_vg(pe, U, c):
            use = Use("l1", U[0], f"vg{c}")
            use.claim(pe)
            for k in range(KT):
                w = WG["vg"] + k * 512
                last = mm3(pe, use.ps[:, :], ln["a"]["h"][:, k, c * P:(c + 1) * P],
                           ln["a"]["l"][:, k, c * P:(c + 1) * P], gh[:, w:w + 512], gl[:, w:w + 512],
                           k == 0, k == KT - 1)
            last.then_inc(S(use.full), 1)

        def l1_out(pe, U, c):
            u = U[0]
            if c % 2 == 0:
                pe.wait_ge(S("l1_acc"), u * 3 + 1 + c // 2)
            o = accA[:, (c % 2) * D:(c % 2 + 1) * D]
            pe.wait_ge(S("l1_st"), u * 8 + 2 * c + 1)
            pe.matmul(o, qp[:, c * P:(c + 1) * P], sd[:, c, :], start=c % 2 == 0, stop=False,
                      skip_group_check=True)
            Use("l1", u, f"A{c}").emptied(pe)
            for h in range(H1):
                last = pe.matmul(o[:, h * DV:(h + 1) * DV], am[:, c, h * P:(h + 1) * P],
                                 vtok[:, c, h * DV:(h + 1) * DV], start=False, stop=c % 2 == 1 and h == H1 - 1,
                                 skip_group_check=True)
            last.then_inc(S("l1_o"), 1)

        def l1_act(act, U, s):
            u, p, q = U
            if s == 0:
                ln_act(act, "l1", u)
            elif s == 1:
                xt_act(act, "l1", u)
            elif s == 2:
                use = Use("l1", u, "low")
                use.filled(act)
                act.activation(low[:, :], use.ps[0:16, :], ACT.Copy).then_inc(S(use.free), 1)
                l1_gate_act(act, U, 0)
            elif s == 3:
                use = Use("l1", u, "zg")
                use.filled(act)
                act.activation(t1[:, 0, :], use.ps[:, :], ACT.Abs, bias=col("gkb", 1)).then_inc(S("l1_ab"), 1)
                act.activation(t2[:, 0, :], use.ps[:, :], ACT.Relu, bias=ngkb[:, 0:1], scale=-1.0)\
                   .then_inc(S(use.free), 1)
                act.wait_ge(S("l1_ab"), u + 1)
                act.activation(t1[:, 0, :], t1[:, 0, :], ACT.Exp, scale=-1.0).then_inc(S("l1_ea"), 1)
                act.wait_ge(S("l1_ea"), u + 1)
                act.activation(t1[:, 0, :], t1[:, 0, :], ACT.Ln, bias=1.0).then_inc(S("l1_la"), 1)
                l1_gate_act(act, U, 1)
            elif s == 4:
                act.wait_ge(S("l1_dm"), u + 1)
                act.activation(dec[:, :], dmid[:, :], ACT.Exp, scale=1.0 / GATE_NORM).then_inc(S("l1_dec"), 1)
                act.wait_ge(S("l1_ex"), u + 1)
                act.activation(t1[:, 0, :], t2[:, 0, :], ACT.Exp, scale=-1.0 / GATE_NORM).then_inc(S("l1_eq"), 1)
                act.activation(t3[:, 0, :], t2[:, 0, :], ACT.Exp, scale=1.0 / GATE_NORM).then_inc(S("l1_ek"), 1)
                l1_gate_act(act, U, 2)
            elif s == 5:
                l1_gate_act(act, U, 3)
            elif s in (10, 12):
                i = (s - 10) // 2
                m = u * 2 + i + 1
                act.wait_ge(S("l1_o"), u * NT + 2 * i + 2)
                act.activation(kf[:, 1, :], accA[:, :], ACT.Square).then_inc(S("l1_sq"), 1)
                act.wait_ge(S("l1_ss"), m)
                act.activation(rr[:, i, :], ss[:, i, :], ACT.Ln, scale=1.0 / DV, bias=cst[:, 0:1])\
                   .then_inc(S("l1_ls"), 1)
                act.wait_ge(S("l1_ls"), m)
                act.activation(rr[:, i, :], rr[:, i, :], ACT.Exp, scale=-0.5).then_inc(S("l1_rr"), 1)
            elif s == 13:
                if isinstance(u, int) and u == 0:
                    Use("l0", NU - 1, "W1").filled(act)
                else:
                    Use("l1", u - 1, "W1").filled(act)
                for f in range(KT):
                    use = Use("l1", u, f"oT{f}")
                    use.filled(act)
                    act.activation(oh[:, f, :], use.ps[:, :], ACT.Copy).then_inc(S("l1_oh"), 1)

        def l1_gate_act(act, U, c):
            u = U[0]
            m = u * NT + c + 1
            use = Use("l1", u, f"vg{c}")
            use.filled(act)
            act.activation(vtok[:, c, :], use.ps[:, 0:D], ACT.Copy).then_inc(S("l1_v"), 1)
            act.activation(gate1[:, c, :], use.ps[:, D:2 * D], ACT.Exp, scale=-1.0).then_inc(S("l1_g1"), 1)
            act.wait_ge(S("l1_g1"), m)
            act.activation(gate1[:, c, :], gate1[:, c, :], ACT.Ln, bias=1.0).then_inc(S("l1_g2"), 1)
            act.wait_ge(S("l1_g2"), m)
            act.activation(gate1[:, c, :], gate1[:, c, :], ACT.Exp, scale=-1.0).then_inc(S("l1_g3"), 1)

        def l1_gate_dve(dve, U, c):
            u = U[0]
            use = Use("l1", u, f"vg{c}")
            dve.wait_ge(S("l1_g3"), u * NT + c + 1)
            dve.tensor_tensor(gate1[:, c, :], gate1[:, c, :], use.ps[:, D:2 * D], ALU.mult)\
               .then_inc(S(use.free), 1)

        def l1_dve(dve, U, s):
            u, p, q = U
            if s == 0:
                dve.wait_ge(S(f"ld{p}"), 16 * (q + 1 + NU // 2))
                ln_dve(dve, "l1", u, x0[:, p])
            elif s == 1:
                norm_dve(dve, "l1", u, x0[:, p])
                xt_dve(dve, "l1", u)
            elif s == 2:
                l1_gate_dve(dve, U, 0)
            elif s == 3:
                dve.wait_ge(S("l1_la"), u + 1)
                Use("l1", u, "zg").emptied(dve)
                dve.tensor_tensor(t1[:, 0, :], t1[:, 0, :], t2[:, 0, :], ALU.add).then_inc(S("l1_nl"), 1)
                dve.wait_ge(S("l1_nl"), u + 1)
                dve.tensor_tensor_scan(t1[:, 0, :], t1[:, 0, :], zeros[:, 0:1].to_broadcast([P, UT]), 0.0,
                                       ALU.add, ALU.add).then_inc(S("l1_cum"), 1)
                dve.wait_ge(S("l1_cum"), u + 1)
                dve.tensor_copy(mid[:, p, 1:NT + 1], t1[:, 0, :].rearrange("p (c t) -> p c t", c=NT)[:, :, P // 2 - 1])\
                   .then_inc(S("l1_mid"), 1)
                dve.wait_ge(S("l1_mid"), u * 2 + 1)
                dve.tensor_tensor(dmid[:, :], mid[:, p, 0:NT], mid[:, p, 1:NT + 1], ALU.subtract)\
                   .then_inc(S("l1_dm"), 1)
                dve.tensor_tensor(t2[:, 0, :].rearrange("p (c t) -> p c t", c=NT),
                                  t1[:, 0, :].rearrange("p (c t) -> p c t", c=NT),
                                  bc(mid[:, p, 1:NT + 1], 2, [P, NT, P]), ALU.subtract).then_inc(S("l1_rel"), 1)
                dve.wait_ge(S("l1_dm"), u + 1)
                dve.tensor_tensor(mid[:, p, 0:1], mid[:, p, NT:NT + 1], t1[:, 0, UT - 1:UT], ALU.subtract)\
                   .then_inc(S("l1_mid"), 1)
                dve.wait_ge(S("l1_rel"), u + 1)
                dve.tensor_scalar(t2[:, 0, :], t2[:, 0, :], SPREAD * GATE_NORM, -SPREAD * GATE_NORM, ALU.min,
                                  ALU.max).then_inc(S("l1_ex"), 1)
                l1_gate_dve(dve, U, 1)
            elif s in (4, 5):
                l1_gate_dve(dve, U, s - 2)
            elif s == 6:
                use = Use("l1", u, "q")
                use.filled(dve)
                dve.wait_ge(S("l1_eq"), u + 1)
                dve.scalar_tensor_tensor(out=qp[:, :], in0=use.ps[:, :], scalar=DK ** -0.5, in1=t1[:, 0, :],
                                         op0=ALU.mult, op1=ALU.mult).then_inc(S(use.free), 1)
                use = Use("l1", u, "k")
                use.filled(dve)
                dve.wait_ge(S("l1_ek"), u + 1)
                dve.tensor_tensor(kf[:, 0, :], use.ps[:, :], t3[:, 0, :], ALU.mult).then_inc(S(use.free), 1)
            elif s == 7:
                dve.wait_ge(S("l1_kt"), u + 1)
                dve.tensor_copy(flat(ktok[:, :, :]), accA[:, :]).then_inc(S("l1_acc"), 1)
                dve.wait_ge(S("l1_dec"), u + 1)
                wait(dve, "l1_st", u * 8)
                l1_decay(dve, U, 0)
            elif 8 <= s <= 12:
                c = s - 8
                if c in (1, 2):
                    use = Use("l1", u, f"dS{c - 1}")
                    use.filled(dve)
                    wait(dve, "l1_st", u * 8 + 1 if c == 1 else u * 8 + 5)
                    dve.tensor_tensor(dst[:, :].rearrange("p (c e) -> p c e", c=2),
                                      use.ps[:, :].rearrange("p (c e) -> p c e", c=2),
                                      bc(col("bd32", D), 1, [P, 2, D]), ALU.mult).then_inc(S(use.free), 1)
                    use.emptied(dve)
                    for i in range(2):
                        cc = 2 * (c - 1) + i
                        m = u * 8 + 2 * cc + 1
                        dve.wait_ge(S("l1_st"), m)
                        dve.tensor_tensor(st1[:, p, :], sd[:, cc, :], dst[:, i * D:(i + 1) * D], ALU.add)\
                           .then_inc(S("l1_st"), 1)
                        if cc < NT - 1:
                            dve.wait_ge(S("l1_st"), m + 1)
                            l1_decay(dve, U, cc + 1)
                if c < NT:
                    use = Use("l1", u, f"A{c}")
                    use.filled(dve)
                    dve.tensor_tensor(am[:, c, :].rearrange("p (h t) -> p h t", h=4),
                                      use.ps[:, :].rearrange("p (h t) -> p h t", h=4),
                                      bc(causal, 1, [P, 4, P]), ALU.mult).then_inc(S(use.free), 1)
                if c in (2, 4):
                    i = c // 2 - 1
                    m = u * 2 + i + 1
                    dve.wait_ge(S("l1_sq"), m)
                    dve.tensor_reduce(ss[:, i, :], kf[:, 1, :].rearrange("p (g v) -> p g v", v=DV),
                                      axis=AX.X, op=ALU.add).then_inc(S("l1_ss"), 1)
                    dve.wait_ge(S("l1_rr"), m)
                    dve.tensor_tensor(t3[:, i, :].rearrange("p (g v) -> p g v", v=DV),
                                      accA[:, :].rearrange("p (g v) -> p g v", v=DV),
                                      bc(rr[:, i, :], 2, [P, 2 * H1, DV]), ALU.mult).then_inc(S("l1_acc"), 1)
            elif s == 13:
                for f in range(KT):
                    use = Use("l1", u, f"oT{f}")
                    dve.wait_ge(S("l1_oh"), u * 2 + f + 1)
                    dve.tensor_tensor(ol[:, f, :], use.ps[:, :], oh[:, f, :], ALU.subtract)\
                       .then_inc(S(use.free), 1)
            elif s == 14:
                wo_dve(dve, "l1", U)

        def l1_decay(dve, U, c):
            dve.tensor_scalar(sd[:, c, :], st1[:, U[1], :], dec[:, c:c + 1], None, ALU.mult)\
               .then_inc(S("l1_st"), 1)

        def l1_pool(pool, U, s):
            u, p, q = U
            if 2 <= s <= 5:
                c = s - 2
                Use("l1", u, f"vg{c}").emptied(pool)
                g = gate1[:, c, :].rearrange("p (h v) -> p h v", v=DV)
                pool.tensor_tensor(g, g, bc(col("gnw", DV), 1, [P, H1, DV]), ALU.mult).then_inc(S("l1_gw"), 1)
            elif 7 <= s <= 10:
                c = s - 7
                Use("l1", u, "q").emptied(pool)
                if c < 2:
                    if isinstance(u, int) and u == 0:
                        Use("l0", NU - 1, f"A1{NT - 1}{c}").filled(pool)
                    else:
                        Use("l1", u - 1, f"A{c + 2}").filled(pool)
                else:
                    Use("l1", u, f"A{c - 2}").filled(pool)
                pool.tensor_tensor(qx[:, c % 2, :, :], bc(qp[:, c * P:(c + 1) * P], 1, [P, 4, P]),
                                   bc(col("hm32", H1), 2, [P, 4, P]), ALU.mult).then_inc(S("l1_qx"), 1)
                if c == 3:
                    l1_gated(pool, U, 0)
            elif s == 12:
                l1_gated(pool, U, 1)

        def l1_gated(pool, U, i):
            u = U[0]
            pool.wait_ge(S("l1_acc"), u * 3 + 2 + i)
            pool.wait_ge(S("l1_gw"), u * NT + 2 * i + 2)
            pool.tensor_tensor(t3[:, i, :], t3[:, i, :], gg[:, i, :], ALU.mult).then_inc(S("l1_on"), 1)

        def moe_pe(pe, U, s):
            u, p, q = U
            first = isinstance(u, int) and u == 0
            if s == 1:
                xt_pe(pe, "moe", u)
            elif s == 2:
                xt_ready(pe, "moe", u)
                if first:
                    pe.wait_ge(S("w_lo"), M2_AT + 1)
                use = Use("moe", u, "rt")
                use.claim(pe)
                for j in range(NT):
                    for k in range(KT):
                        c = W2["router"] + k * NE
                        last = mm3(pe, use.ps[:, j * NE:(j + 1) * NE], ln["b"]["h"][:, k, j * P:(j + 1) * P],
                                   ln["b"]["l"][:, k, j * P:(j + 1) * P], mh[:, c:c + NE], ml[:, c:c + NE],
                                   j == 0 and k == 0, j == NT - 1 and k == KT - 1)
                last.then_inc(S(use.full), 1)
            elif s == 3:
                use = Use("moe", u, "cT")
                use.claim(pe)
                pe.wait_ge(S("moe_cw"), u + 1)
                for j in range(NT):
                    last = pe.transpose(use.ps[0:2 * NE, j * P:(j + 1) * P], cwr[:, j, :].bitcast(f32), ident)
                last.then_inc(S(use.full), 1)
            elif 4 <= s <= 14:
                e = s - 4
                if e <= NE:
                    if first:
                        end = W2[f"wd{e}"] + D
                        pe.wait_ge(S("w_lo"), M2_AT + (end + PIECE - 1) // PIECE)
                    for n in "gu":
                        use = Use("moe", u, f"{n}{e}")
                        use.claim(pe)
                        proj(pe, use.ps[:, :], "b", mh, ml, W2[f"w{n}{e}"], IE, IE).then_inc(S(use.full), 1)
                if e < NE:
                    use = Use("moe", u, f"c{e}")
                    use.claim(pe)
                    Use("moe", u, "cT").emptied(pe)
                    pe.matmul(use.ps[:, :], selr[:, e:e + 1].to_broadcast([2 * NE, P]), cT[:, :], start=True,
                              stop=True).then_inc(S(use.full), 1)
                if e >= 2:
                    pe.wait_ge(S("moe_hl"), u * (NE + 1) + e - 1)
                    down_pe(pe, "moe", u, e - 2, NE + 1, W2[f"wd{e - 2}"], "moe_dn")

        def moe_act(act, U, s):
            u, p, q = U
            if s == 0:
                ln_act(act, "moe", u)
            elif s == 1:
                xt_act(act, "moe", u)
            elif s == 2:
                use = Use("moe", u, "rt")
                use.filled(act)
                act.activation(flat(sc[:, :, :]), use.ps[:, 0:NT * NE], ACT.Exp, scale=-1.0)\
                   .then_inc(S(use.free), 1)
            elif 4 <= s <= 13:
                e = s - 4
                n = u * (NE + 1) + e
                if e >= 1:
                    moe_h_ready(act, u, e - 1)
                    wait(act, "moe_dn", n - min(e, 2))
                    act.activation(hh[:, (e - 1) % 2, :], hfull[:, (e - 1) % 2, :], ACT.Copy)\
                       .then_inc(S("moe_hh"), 1)
                if e <= NE:
                    use = Use("moe", u, f"g{e}")
                    use.filled(act)
                    act.activation(sg[:, e % 2, :], use.ps[:, :], ACT.Exp, scale=-1.0).then_inc(S("moe_e1"), 1)
                    act.wait_ge(S("moe_e1"), n + 1)
                    act.activation(sg[:, e % 2, :], sg[:, e % 2, :], ACT.Ln, bias=1.0).then_inc(S("moe_e2"), 1)
                    act.wait_ge(S("moe_e2"), n + 1)
                    act.activation(sg[:, e % 2, :], sg[:, e % 2, :], ACT.Exp, scale=-1.0)\
                       .then_inc(S("moe_sg"), 1)

        ROUTE = 16

        def route_dve(dve, u):
            k = [0]

            def link(ins):
                k[0] += 1
                ins.then_inc(S("moe_rt"), 1)
                dve.wait_ge(S("moe_rt"), u * ROUTE + k[0])

            v4 = sc4[:, :, :].rearrange("p t (g e) -> p (t g) e", g=2)
            scf, sc4f = flat(sc[:, :, :]), flat(sc4[:, :, :])
            link(dve.tensor_scalar(scf, scf, 1.0, None, ALU.add))
            link(dve.reciprocal(scf, scf))
            link(dve.tensor_tensor(sc4[:, :, :], sc[:, :, :], bc(col("cbias", NE), 1, [P, NT, NE]), ALU.add))
            link(dve.tensor_tensor(pr[:, :, 0:3], v4[:, :, 0:3], v4[:, :, 1:4], ALU.add))
            link(dve.tensor_tensor(pr[:, :, 3:5], v4[:, :, 0:2], v4[:, :, 2:4], ALU.add))
            link(dve.tensor_tensor(pr[:, :, 5:6], v4[:, :, 0:1], v4[:, :, 3:4], ALU.add))
            link(dve.tensor_reduce(flat(gs[:, :, :]), pr[:, :, :], axis=AX.X, op=ALU.max))
            link(dve.tensor_tensor(gm[:, :, 0], gs[:, :, 0], gs[:, :, 1], ALU.is_ge))
            link(dve.tensor_tensor(gm[:, :, 1], gs[:, :, 0], gs[:, :, 1], ALU.is_lt))
            link(dve.tensor_tensor(v4, v4, bc(flat(gm[:, :, :]), 2, [P, 2 * NT, NE // 2]), ALU.mult))
            mj = bc(sc4[:, :, :], 2, [P, NT, NE, NE])
            mi = bc(sc4[:, :, :], 3, [P, NT, NE, NE])
            link(dve.tensor_tensor(cmp1[:, :, :, :], mj, mi, ALU.is_gt))
            link(dve.tensor_tensor(cmp2[:, :, :, :], mj, mi, ALU.is_equal))
            c1 = cmp1[:, :, :, :].rearrange("p t i j -> p t (i j)")
            c2 = cmp2[:, :, :, :].rearrange("p t i j -> p t (i j)")
            link(dve.tensor_tensor(c2, c2, bc(col("tri", NE * NE), 1, [P, NT, NE * NE]), ALU.mult))
            link(dve.tensor_tensor(c1, c1, c2, ALU.add))
            link(dve.tensor_reduce(flat(rk[:, :, :]), cmp1[:, :, :, :].rearrange("p t i j -> p (t i) j"),
                                   axis=AX.X, op=ALU.add))
            link(dve.scalar_tensor_tensor(out=flat(cw[:, :, :]), in0=flat(rk[:, :, :]), scalar=1.5, in1=scf,
                                          op0=ALU.is_lt, op1=ALU.mult))
            assert k[0] == ROUTE
            dve.tensor_reduce(dn[:, 0, :], cw[:, :, :], axis=AX.X, op=ALU.add).then_inc(S("moe_ds"), 1)
            dve.wait_ge(S("moe_ds"), u * 2 + 1)
            dve.tensor_scalar(dn[:, 1, :], dn[:, 0, :], 1e-20, None, ALU.add).then_inc(S("moe_ds"), 1)
            dve.wait_ge(S("moe_ds"), u * 2 + 2)
            dve.reciprocal(dn[:, 0, :], dn[:, 1, :]).then_inc(S("moe_rd"), 1)
            dve.wait_ge(S("moe_rd"), u + 1)
            dve.tensor_tensor(cw[:, :, :], cw[:, :, :], bc(dn[:, 0, :], 2, [P, NT, NE]), ALU.mult)\
               .then_inc(S("moe_nw"), 1)
            dve.wait_ge(S("moe_nw"), u + 1)
            dve.tensor_copy(cwr[:, :, 0:NE], cw[:, :, :]).then_inc(S("moe_ch"), 1)
            dve.wait_ge(S("moe_ch"), u + 1)
            dve.tensor_tensor(cwr[:, :, NE:2 * NE], cw[:, :, :], cwr[:, :, 0:NE], ALU.subtract)\
               .then_inc(S("moe_cw"), 1)

        def moe_dve(dve, U, s):
            u, p, q = U
            if s == 0:
                x1_ready(dve, "l1", u)
                ln_dve(dve, "moe", u, x1[:, p])
            elif s == 1:
                norm_dve(dve, "moe", u, x1[:, p])
                xt_dve(dve, "moe", u)
            elif s == 2:
                Use("moe", u, "rt").emptied(dve)
                route_dve(dve, u)
            elif s == 3:
                use = Use("moe", u, "cT")
                use.filled(dve)
                dve.tensor_copy(cT[:, :], use.ps[0:2 * NE, :]).then_inc(S(use.free), 1)
            elif 4 <= s <= 12:
                e = s - 4
                n = u * (NE + 1) + e
                h = hfull[:, e % 2, :]
                wait(dve, "moe_hl", n - min(e, 1))
                if isinstance(u, int) and u == 0 and e < 2:
                    dve.wait_ge(S("ffn_hl"), at("ffn_hl", NU * NF))
                use = Use("moe", u, f"g{e}")
                dve.wait_ge(S("moe_sg"), n + 1)
                dve.tensor_tensor(h, sg[:, e % 2, :], use.ps[:, :], ALU.mult).then_inc(S(use.free), 1)
                use.emptied(dve)
                use = Use("moe", u, f"u{e}")
                use.filled(dve)
                if e < NE:
                    dve.tensor_tensor(sg[:, e % 2, :], h, use.ps[:, :], ALU.mult).then_inc(S(use.free), 1)
                    use.emptied(dve)
                    use = Use("moe", u, f"c{e}")
                    use.filled(dve)
                    dve.tensor_tensor(h, sg[:, e % 2, :], use.ps[:, :], ALU.mult).then_inc(S(use.free), 1)
                else:
                    dve.tensor_tensor(h, h, use.ps[:, :], ALU.mult).then_inc(S(use.free), 1)
            elif s == 15:
                dve.wait_ge(S("moe_dn"), u * (NE + 1) + NE + 1)
                resid_dve(dve, U)

        def moe_h_ready(eng, u, e):
            Use("moe", u, f"c{e}" if e < NE else f"u{e}").emptied(eng)

        def moe_pool(pool, U, s):
            u, p, q = U
            if 5 <= s <= 13:
                e = s - 5
                n = u * (NE + 1) + e
                pool.wait_ge(S("moe_hh"), n + 1)
                pool.tensor_tensor(hl[:, e % 2, :], hfull[:, e % 2, :], hh[:, e % 2, :], ALU.subtract)\
                    .then_inc(S("moe_hl"), 1)

        N_STEPS = {"l0": 20, "ffn": 12, "l1": 15, "moe": 16}

        ORDER = {
            "l0": "a2 b0 a3 b1 a4 a5 a6 b2 b3 b4 a7 a8 b5 a9 b6 a10 a11 b7 a12 a13 b8 a14 b9 a15 a16 b10 c0 a17 a18 "
                  "c1 b11 a19",
            "l1": "a2 b0 b1 a3 b2 a4 a5 b3 a6 b4 a7 b5 a8 b6 a9 b7 a10 b8 a11 b9 a12 c0 b10 a13 c1 b11 a14 "
                  "b12 b13 b14 b15",
        }

        def beside(a, ua, b, ub, uc):
            units = {"a": (a, ua), "b": (b, ub), "c": (a, uc)}
            return [(*units[x_[0]], int(x_[1:])) for x_ in ORDER[a].split() if units[x_[0]][1] is not None]

        def unit(u):
            return (u, u % 2, u // 2)

        def program(eng, fns, prep, edge):
            def run(steps):
                for kind, U, s in steps:
                    fns[kind](eng, U, s)

            def phase(a, b, after):
                edge(a, "start", None)
                for n, (kind, U, s) in enumerate([(a, unit(0), 0), (a, unit(0), 1)]
                                                 + beside(a, unit(0), b, None, unit(1))):
                    for i in after.get(n, ()):
                        prep(i)
                    fns[kind](eng, U, s)
                with eng.Fori(0, (NU - 2) // 2) as i:
                    for r in range(2):
                        edge(a, "round", (2 * i + r, r, i))
                        run(beside(a, (2 * i + r + 1, 1 - r, i + r), b, (2 * i + r, r, i), (2 * i + r + 2, r, i + 1)))
                        edge(b, "stored", (2 * i + r, r, i))
                run(beside(a, unit(NU - 1), b, unit(NU - 2), None))
                edge(b, "stored", unit(NU - 2))
                edge(b, "tables", None)
                run([(b, unit(NU - 1), s) for s in range(N_STEPS[b])])
                edge(b, "stored", unit(NU - 1))

            phase("l0", "ffn", {2: range(L0_PIECES)}
                  | {8 + i: [L0_PIECES + i] for i in range(M1_PIECES - L0_PIECES + G_PIECES)})
            phase("l1", "moe", {2 + i: [M2_AT + i] for i in range(M2_PIECES)})

        PIECES = [(wm1, mh, ml, a, n) for a, n in pieces(W1_COLS)] + [(wg, gh, gl, a, n) for a, n in pieces(WG_COLS)] \
            + [(wm2, mh, ml, a, n) for a, n in pieces(W2_COLS)]
        M1_PIECES, G_PIECES, M2_PIECES = (len(pieces(c)) for c in (W1_COLS, WG_COLS, W2_COLS))
        M2_AT = M1_PIECES + G_PIECES
        L0_PIECES = -(-W1["w1"] // PIECE)
        N_INIT = 8

        def nothing(*_):
            pass

        block = ctx.enter_context(nc.Block())

        @block.sync
        def _(sp):
            def load(src, U, wait_on=None):
                u, p, q = U
                sp.dma_start(x0[:, p, :, :], src[bass.ds(u, 1)].rearrange("a p j d -> p (a j) d"))\
                  .then_inc(S(f"ld{p}"), 16)

            def piece(i):
                if i >= 2:
                    sp.wait_ge(S("w_lo"), i - 1)
                src, _, _, a, n = PIECES[i]
                sp.dma_start(stage[:, i % 2, 0:n], src[:, a:a + n]).then_inc(S(f"w_ld{i % 2}"), 16)

            def edge(kind, what, U):
                if what == "start" and kind == "l1":
                    for p in range(2):
                        sp.wait_ge(S(f"sto{p}"), at(f"sto{p}", 16 * (NU // 2)))
                        load(scratch, unit(p))
                elif what == "round":
                    u, p, q = U
                    x1_ready(sp, kind, u)
                    load(x if kind == "l0" else scratch, (u + 2, p, q))
                elif what == "stored":
                    u, p, q = U
                    sp.wait_ge(S("accB_free"), at("accB_free", seq(kind, u) * 2 + 2))
                    dst_ = scratch if kind == "ffn" else out
                    sp.dma_start(dst_[bass.ds(u, 1)].rearrange("a p j d -> p (a j) d"), x1[:, p, :, :])\
                      .then_inc(S(f"sto{p}"), 16)

            sp.dma_start(sm[:, :], small).then_inc(S("ld_sm"), 16)
            load(x, unit(0))
            load(x, unit(1))
            steps = {k: nothing for k in N_STEPS}
            program(sp, steps, piece, edge)
            for p in range(2):
                sp.wait_ge(S(f"sto{p}"), at(f"sto{p}", 16 * NU))

        @block.gpsimd
        def _(pool):
            for t in (st0, cum, st1, mid, zeros, vx):
                pool.memset(t[tuple(slice(None) for _ in t.shape)], 0.0).then_inc(S("init"), 1)
            pool.memset(cst[:, 0:1], EPS).then_inc(S("init"), 1)
            pool.memset(cst[:, 1:2], GCLIP).then_inc(S("init"), 1)
            for i, name in enumerate(START_AT_ONE):
                pool.memset(cst[:, i + 2:i + 3], 0.0).then_inc(S(name), 1)
            pool.wait_ge(S("init"), N_INIT)
            pool.wait_ge(S("ld_sm"), 16)
            program(pool, {"l0": l0_pool, "ffn": ffn_pool, "l1": l1_pool, "moe": moe_pool}, nothing, nothing)

        @block.scalar
        def _(act):
            act.wait_ge(S("ld_sm"), 16)
            act.wait_ge(S("init"), N_INIT)
            act.activation(ngkb[:, :], col("gkb", 1), ACT.Copy, scale=-1.0).then_inc(S("ngkb"), 1)
            act.wait_ge(S("ngkb"), 1)

            def split_high(i):
                act.wait_ge(S(f"w_ld{i % 2}"), 16 * (i // 2 + 1))
                if i == M2_AT:
                    act.wait_ge(S("ffn_dn"), at("ffn_dn", NU * NF))
                    Use("l0", NU - 1, "W1").filled(act)
                _, hi, lo, a, n = PIECES[i]
                act.activation(hi[:, a:a + n], stage[:, i % 2, 0:n], ACT.Copy).then_inc(S("w_hi"), 1)

            def edge(kind, what, U):
                if what == "start" or what == "tables" and kind == "ffn":
                    act.preload_act_table_set("natural_log_exp_and_others")

            program(act, {"l0": l0_act, "ffn": ffn_act, "l1": l1_act, "moe": moe_act}, split_high, edge)

        @block.vector
        def _(dve):
            dve.wait_ge(S("init"), N_INIT)
            dve.wait_ge(S("ld_sm"), 16)
            dve.tensor_copy(selr[:, :], col("sel", NE, 16)).then_inc(S("selr"), 1)

            def split_low(i):
                _, hi, lo, a, n = PIECES[i]
                dve.wait_ge(S("w_hi"), i + 1)
                dve.tensor_tensor(lo[:, a:a + n], stage[:, i % 2, 0:n], hi[:, a:a + n], ALU.subtract)\
                   .then_inc(S("w_lo"), 1)

            program(dve, {"l0": l0_dve, "ffn": ffn_dve, "l1": l1_dve, "moe": moe_dve}, split_low, nothing)

        @block.tensor
        def _(pe):
            pe.wait_ge(S("ld_sm"), 16)
            pe.wait_ge(S("selr"), 1)
            program(pe, {"l0": l0_pe, "ffn": ffn_pe, "l1": l1_pe, "moe": moe_pe}, nothing, nothing)


def kernel(**inputs):
    import numpy as np
    import concourse.bacc as bacc
    from concourse.bass_utils import run_bass_kernel_spmd

    a = {k: np.asarray(v) for k, v in inputs.items()}
    f32 = np.float32

    def ktiles(w):
        k, n = w.shape
        return w.reshape(k // P, P, n).transpose(1, 0, 2).reshape(P, -1)

    def pack(cols, at, parts):
        out = np.zeros((P, cols), f32)
        for name, w in parts.items():
            out[0:w.shape[0], at[name]:at[name] + w.shape[1]] = w
        return out

    def block_diag(row):
        out = np.zeros((HH, D0, HH, D0), f32)
        for h in range(HH):
            out[h, :, h, :] = row.reshape(D0, 1)
        return out.reshape(P, P)

    wm1 = pack(W1_COLS, W1, {
        "k": ktiles(a["L0_attn_Wk"].T), "q": ktiles(a["L0_attn_Wq"].T), "v": ktiles(a["L0_attn_Wv"].T),
        "o": ktiles(a["L0_attn_Wo"].T), "gate": block_diag(a["L0_attn_gw"]),
        "w1": ktiles(a["L0_ffn_w1"]), "w2": ktiles(a["L0_ffn_w2"])})
    experts = {"router": ktiles(a["L1_ffn_router_weight"].T)}
    for e in range(NE + 1):
        for n, name in (("wg", "gate"), ("wu", "up"), ("wd", "down")):
            w = a[f"L1_ffn_w_{name}"][e] if e < NE else a[f"L1_ffn_sw_{name}"]
            experts[f"{n}{e}"] = ktiles(w)
    wm2 = pack(W2_COLS, W2, experts)
    vg = np.concatenate([a["L1_attn_Wv"], a["L1_attn_Wg"]], axis=1)
    wg = pack(WG_COLS, WG, {"q": ktiles(a["L1_attn_Wq"]), "k": ktiles(a["L1_attn_Wk"]), "vg": ktiles(vg),
                            "w1": ktiles(a["L1_attn_gk_w1"]), "o": ktiles(a["L1_attn_Wo"])})
    r = np.arange(P)
    e = np.arange(NE)
    sel = np.zeros((P, NE), f32)
    sel[e, e] = 1
    sel[NE + e, e] = 1
    small = pack(SM_COLS, SM, {
        "swbd": block_diag(a["L0_attn_sw"]), "gkw2": a["L1_attn_gk_w2"], "ident": np.eye(P, dtype=f32),
        "causal": (r[:, None] <= r[None, :]).astype(f32),
        "bd16": (r[:, None] // D0 == r[None, :] // D0).astype(f32),
        "bd32": (r[:, None] // DK == np.arange(D)[None, :] // DV).astype(f32),
        "hm16": (r[:, None] // D0 == np.arange(HH)[None, :]).astype(f32),
        "hm32": (r[:, None] // DK == np.arange(H1)[None, :]).astype(f32),
        "tri": np.broadcast_to((e[:, None] > e[None, :]).astype(f32).reshape(1, -1), (P, NE * NE)),
        "sel": sel, "b1": a["L0_ffn_b1"].reshape(NF, P).T, "gkb": a["L1_attn_gk_b2"].reshape(P, 1),
        "gnw": np.broadcast_to(a["L1_attn_g_norm_w"], (P, DV)), "b2": np.broadcast_to(a["L0_ffn_b2"], (P, D)),
        "cbias": np.broadcast_to(a["L1_ffn_correction_bias"], (P, NE))})
    xs = a["L0_attn_x"].reshape(B, NU // B, NT, P, D).transpose(1, 0, 3, 2, 4).reshape(NU, P, NT, D)

    arrays = {"x": np.ascontiguousarray(xs), "wm1": wm1, "wm2": wm2, "wg": wg, "small": small}
    nc = bacc.Bacc("TRN2", target_bir_lowering=False, num_devices=1)
    dt = mybir.dt.float32
    args = [nc.dram_tensor(f"in_{k}", v.shape, dt, kind="ExternalInput").ap() for k, v in arrays.items()]
    scratch = nc.dram_tensor("between", (NU, P, NT, D), dt, kind="Internal").ap()
    out = nc.dram_tensor("out", (NU, P, NT, D), dt, kind="ExternalOutput").ap()
    build(nc, *args, scratch, out)
    res = run_bass_kernel_spmd(nc, [{f"in_{k}": v for k, v in arrays.items()}], core_ids=[0])
    got = np.asarray(res.results[0]["out"])
    return got.reshape(NU // B, B, P, NT, D).transpose(1, 0, 3, 2, 4).reshape(B, L, D)
```

```python
import concourse.bass as bass
from concourse import mybir
from contextlib import ExitStack

P = 128
B, L, D = 2, 2048, 256
UT = 512
NT = UT // P
NU = B * L // UT
KT = D // P
F1 = 1024
NF = F1 // P
H0, D0 = 16, 16
HH = P // D0
H1, DK, DV = 4, 32, 64
NE, IE = 8, 128
EPS = 1e-5
GCLIP = 1e-6
LOG_GCLIP = -13.815510557964274
GATE_NORM = 16.0
SPREAD = 43.0


def layout(parts):
    at, out = 0, {}
    for name, cols in parts:
        out[name] = at
        at += cols
    return out, at


W1, W1_COLS = layout([("k", KT * D), ("gate", P), ("v", KT * D), ("q", KT * D), ("o", KT * D),
                      ("w1", KT * F1), ("w2", NF * D)])
W2, W2_COLS = layout([("router", KT * NE)]
                     + [(f"{n}{e}", KT * IE) for e in range(NE + 1) for n in ("wg", "wu", "wd")])
WG, WG_COLS = layout([("q", KT * 128), ("k", KT * 128), ("vg", KT * 512), ("o", KT * D)])
GK, G_COLS = WG_COLS, WG_COLS + KT * 128
GK_RANK, GK_RAW = 16, D + 128
SM, SM_COLS = layout([("swbd", P), ("ident", P), ("causal", P), ("bd16", P), ("bd32", D),
                      ("hm16", HH), ("hm32", H1), ("tri", NE * NE), ("sel", NE), ("b1", NF), ("gkb", 1),
                      ("gnw", DV), ("b2", D), ("cbias", NE)])
PIECE = 512


def pieces(cols):
    return [(a, min(PIECE, cols - a)) for a in range(0, cols, PIECE)]


def _l0_uses():
    out = ["K0", "Z0", "K1", "Z1", "R0", "V0", "R1", "V1"]
    for hf in range(2):
        out += [f"Q{hf}", f"KT{hf}", f"dS{hf}"] + [f"A{hf}{c}{g}" for c in range(NT) for g in range(2)]
    return out + ["xT0", "xT1", "W0", "W1"]


USES = {
    "l0": _l0_uses(),
    "ffn": ["xT00", "xT01", "xT10", "xT11"] + [f"h{j}" for j in range(NF)],
    "l1": ["zg", "vg0", "vg1", "vg2", "vg3", "q", "k", "KT", "A0", "dS0", "A1", "dS1", "A2", "A3", "oT0", "oT1",
           "xT0", "xT1", "W0", "W1"],
    "moe": ["xT0", "xT1", "rt", "g0", "u0", "cT", "c0"] + [f"{n}{e}" for e in range(1, NE) for n in "guc"]
           + ["g8", "u8"],
}
RING = {"l0": 2, "l1": 2, "ffn": 3, "moe": 3}
for _s, _u in USES.items():
    assert len(_u) % RING[_s] == 0


def build(nc, x, wm1, wm2, wg, wgk, small, scratch, out):
    f32, f32r = mybir.dt.float32, mybir.dt.float32r
    ALU = mybir.AluOpType
    ACT = mybir.ActivationFunctionType
    AX = mybir.AxisListType
    ctx = ExitStack()
    with ctx:
        def sb(name, shape, dt=f32):
            return ctx.enter_context(nc.sbuf_tensor(name, shape, dt))

        sems = {}

        def S(name):
            if name not in sems:
                sems[name] = ctx.enter_context(nc.semaphore(name))
            return sems[name]

        START_AT_ONE = ["free_A0", "free_A1", "free_B0", "free_B1", "free_B2", "accB_free", "ffn_hl", "ffn_dn",
                        "sto0", "sto1"]

        def at(name, n):
            return n + 1 if name in START_AT_ONE else n

        def wait(eng, name, n):
            if not (isinstance(n, int) and n <= 0):
                eng.wait_ge(S(name), at(name, n))

        MCOLS = max(W1_COLS, W2_COLS)
        mh, ml = sb("mh", [P, MCOLS], f32r), sb("ml", [P, MCOLS], f32r)
        gh, gl = sb("gh", [P, G_COLS], f32r), sb("gl", [P, G_COLS], f32r)
        sm = sb("sm", [P, SM_COLS])
        selr = sb("selr", [2 * NE, NE], f32r)
        stage = sb("stage", [P, 2, PIECE])
        cst = sb("cst", [P, 16])
        ngkb = sb("ngkb", [P, 1])
        zeros = sb("zeros", [P, 1])
        x0, x1 = sb("x0", [P, 2, NT, D]), sb("x1", [P, 2, NT, D])
        ln = {}
        for t in "ab":
            ln[t] = dict(st=sb(f"st_{t}", [P, NT, 6]), mv=sb(f"mv_{t}", [P, NT, 2]),
                         df=sb(f"df_{t}", [P, NT]), rs=sb(f"rs_{t}", [P, NT]),
                         xn=sb(f"xn_{t}", [P, 2, D]), h=sb(f"xh_{t}", [P, KT, UT], f32r),
                         l=sb(f"xl_{t}", [P, KT, UT], f32r))
        kf, gg = sb("kf", [P, 2, UT]), sb("gg", [P, 2, UT])
        t1, t2, t3 = sb("t1", [P, 2, UT]), sb("t2", [P, 1, UT]), sb("t3", [P, 2, UT])
        qp = sb("qp", [P, UT])
        qxh, qxl = sb("qxh", [P, 2, 4 * P], f32r), sb("qxl", [P, 2, 4 * P], f32r)
        VX = 4 * (P + D0)
        vx = sb("vx", [P, 2, VX + 64])
        vtok = sb("vtok", [P, NT, D])
        ktok = sb("ktok", [P, NT, P])
        am = sb("am", [P, 4, UT])
        dst = sb("dst", [P, UT])
        st0 = sb("st0", [P, B, 2, P])
        sx = sb("sx", [P, NT - 1, P])
        cum = sb("cum", [P, B, 2])
        oh, ol = sb("oh", [P, KT, UT], f32r), sb("ol", [P, KT, UT], f32r)
        st1 = sb("st1", [P, B, D])
        sd = sb("sd", [P, NT, D])
        mid = sb("mid", [P, B, NT + 1])
        dec = sb("dec", [P, NT])
        dmid = sb("dmid", [P, NT])
        qh, ql = sb("qh", [P, UT], f32r), sb("ql", [P, UT], f32r)
        ss, rr = sb("ss", [P, 2, NT * 2]), sb("rr", [P, 2, NT * 2])
        hfull = sb("hfull", [P, 2, UT])
        hh, hl = sb("hh", [P, 2, UT], f32r), sb("hl", [P, 2, UT], f32r)
        sg = sb("sg", [P, 2, UT])
        sc, sc4 = sb("sc", [P, NT, NE]), sb("sc4", [P, NT, NE])
        pr, gs, gm = sb("pr", [P, NT * 2, 6]), sb("gs", [P, NT, 2]), sb("gm", [P, NT, 2])
        cmp1, cmp2 = (st0[:, b, :, :].rearrange("p f (t i j) -> p (f t) i j", i=NE, j=NE) for b in range(B))
        rk, cw = sb("rk", [P, NT, NE]), sb("cw", [P, NT, NE])
        dn = sb("dn", [P, 2, NT])
        cwr = sb("cwr", [P, NT, 2 * NE], f32r)

        psA = [ctx.enter_context(nc.psum_tensor(f"psA{i}", [P, UT], f32)) for i in range(2)]
        accA = ctx.enter_context(nc.psum_tensor("accA", [P, UT], f32))
        psB = [ctx.enter_context(nc.psum_tensor(f"psB{i}", [P, UT], f32)) for i in range(3)]
        accB = [ctx.enter_context(nc.psum_tensor(f"accB{i}", [P, UT], f32)) for i in range(2)]

        gk_ps = accB[0][:, 0:KT * P]

        def col(name, n, rows=P):
            return sm[0:rows, SM[name]:SM[name] + n]

        ident, causal = col("ident", P), col("causal", P)

        kh, kl = oh[:, 1, :], ol[:, 1, :]
        cT = ql[0:2 * NE, :]
        qx1 = vx[:, :, 0:4 * P]
        gate1 = gg[:, :, :].rearrange("p a (b d) -> p (a b) d", d=D)
        on1 = t3[:, :, :].rearrange("p a (b d) -> p (a b) d", d=D)

        class Use:

            def __init__(self, kind, u, name):
                n, i = RING[kind], USES[kind].index(name)
                phase2 = kind in ("l1", "moe")
                before = NU * len(USES["l0" if n == 2 else "ffn"]) // n if phase2 else 0
                self.n = before + u * (len(USES[kind]) // n) + i // n
                if n == 2:
                    if name[0] == "x":
                        self.n = before if isinstance(u, int) and u == 0 \
                            else before + 1 + (u - 1) * (len(USES[kind]) // n) + i // n
                    elif not (isinstance(u, int) and u == NU - 1 and name[0] == "W"):
                        self.n = self.n + 1
                self.ps = (psA if n == 2 else psB)[i % n]
                ring = "A" if n == 2 else "B"
                self.full, self.free = f"full_{ring}{i % n}", f"free_{ring}{i % n}"

            def claim(self, eng):
                wait(eng, self.free, self.n)

            def filled(self, eng):
                eng.wait_ge(S(self.full), self.n + 1)

            def emptied(self, eng):
                eng.wait_ge(S(self.free), at(self.free, self.n + 1))

        STREAM = {"l0": "a", "l1": "a", "ffn": "b", "moe": "b"}
        LAST_XT = {"l0": "Q1", "ffn": f"h{NF - 1}", "l1": "k", "moe": "u8"}

        def seq(kind, u):
            return (NU if kind in ("l1", "moe") else 0) + u

        def xt_unused(eng, kind, u):
            if kind == "ffn":
                wait(eng, "ffn_dn", u * NF)
            elif isinstance(u, int) and u == 0:
                if kind in ("l1", "moe"):
                    k = "l0" if kind == "l1" else "ffn"
                    Use(k, NU - 1, LAST_XT[k]).filled(eng)
            else:
                Use(kind, u - 1, LAST_XT[kind]).filled(eng)

        def bc(ap, axis, shape):
            return ap.unsqueeze(axis).to_broadcast(shape)

        def heads(ap):
            return ap.rearrange("p (h t) -> p h t", h=4)

        def flat(ap):
            return ap.rearrange("p a b -> p (a b)")

        def mm3(pe, psum, wh, wl, xh, xl, first, last):
            pe.matmul(psum, wh, xh, start=first, stop=False, skip_group_check=True)
            pe.matmul(psum, wh, xl, start=False, stop=False, skip_group_check=True)
            return pe.matmul(psum, wl, xh, start=False, stop=last, skip_group_check=True)

        def proj(pe, psum, t, wh, wl, at, stride, m):
            for k in range(KT):
                c = at + k * stride
                last = mm3(pe, psum, wh[:, c:c + m], wl[:, c:c + m], ln[t]["h"][:, k, :], ln[t]["l"][:, k, :],
                           k == 0, k == KT - 1)
            return last

        def ln_stats(dve, kind, xsrc, tiles):
            t = STREAM[kind]
            for j in tiles:
                dve.bn_stats(ln[t]["st"][:, j, :], xsrc[:, j, :]).then_inc(S(f"bn_{t}"), 1)

        def ln_dve(dve, kind, u):
            t, n = STREAM[kind], seq(kind, u)
            d = ln[t]
            st, mv, df = d["st"], d["mv"], d["df"]
            dve.wait_ge(S(f"bn_{t}"), n * NT + NT)
            dve.tensor_tensor(df[:, :], st[:, :, 1], st[:, :, 4], ALU.subtract).then_inc(S(f"df_{t}"), 1)
            dve.tensor_tensor(mv[:, :, 0], st[:, :, 1], st[:, :, 4], ALU.add).then_inc(S(f"sm_{t}"), 1)
            dve.tensor_tensor(mv[:, :, 1], st[:, :, 2], st[:, :, 5], ALU.add).then_inc(S(f"m2_{t}"), 1)
            dve.wait_ge(S(f"df_{t}"), n * 2 + 1)
            dve.tensor_tensor(df[:, :], df[:, :], df[:, :], ALU.mult).then_inc(S(f"df_{t}"), 1)
            dve.wait_ge(S(f"sm_{t}"), n * 2 + 1)
            dve.tensor_scalar(mv[:, :, 0], mv[:, :, 0], 0.5, None, ALU.mult).then_inc(S(f"sm_{t}"), 1)
            dve.wait_ge(S(f"m2_{t}"), n + 1)
            dve.wait_ge(S(f"df_{t}"), n * 2 + 2)
            dve.scalar_tensor_tensor(out=mv[:, :, 1], in0=df[:, :], scalar=D / 4.0, in1=mv[:, :, 1], op0=ALU.mult,
                                     op1=ALU.add).then_inc(S(f"mv_{t}"), 1)

        def norm_dve(dve, kind, U, tiles):
            u, p, q = U
            t, n = STREAM[kind], seq(kind, u)
            xsrc = (x0 if t == "a" else x1)[:, p]
            d = ln[t]
            dve.wait_ge(S(f"sm_{t}"), n * 2 + 2)
            dve.wait_ge(S(f"rs_{t}"), n + 1)
            for j in tiles:
                if j >= 2:
                    if kind == "ffn":
                        Use(kind, u, "xT01").filled(dve)
                    else:
                        dve.wait_ge(S(f"tp_{kind}"), u * 2 + j - 1)
                dve.tensor_scalar(d["xn"][:, j % 2, :], xsrc[:, j, :], d["mv"][:, j, 0:1], d["rs"][:, j:j + 1],
                                  ALU.subtract, ALU.mult).then_inc(S(f"xn_{t}"), 1)

        def ln_act(act, kind, u):
            t, n = STREAM[kind], seq(kind, u)
            d = ln[t]
            act.wait_ge(S(f"mv_{t}"), n + 1)
            act.activation(d["rs"][:, :], d["mv"][:, :, 1], ACT.Ln, bias=cst[:, 0:1], scale=1.0 / D)\
               .then_inc(S(f"lv_{t}"), 1)
            act.wait_ge(S(f"lv_{t}"), n + 1)
            act.activation(d["rs"][:, :], d["rs"][:, :], ACT.Exp, scale=-0.5).then_inc(S(f"rs_{t}"), 1)

        def xt_names(kind):
            if kind == "ffn":
                return [(f"xT{h}{f}", f, 2 * h, 2) for h in range(2) for f in range(KT)]
            return [(f"xT{f}", f, 0, NT) for f in range(KT)]

        def xt_pe(pe, kind, u):
            t, n = STREAM[kind], seq(kind, u)
            for j in range(NT):
                for name, f, j0, nj in xt_names(kind):
                    if not j0 <= j < j0 + nj:
                        continue
                    use = Use(kind, u, name)
                    if j == j0:
                        use.claim(pe)
                    if f == 0:
                        pe.wait_ge(S(f"xn_{t}"), n * NT + j + 1)
                    last = pe.transpose(use.ps[:, (j - j0) * P:(j - j0 + 1) * P],
                                        ln[t]["xn"][:, j % 2, f * P:(f + 1) * P], ident)
                    if j == j0 + nj - 1:
                        last.then_inc(S(use.full), 1)
                    elif f == KT - 1 and kind != "ffn" and j < 2:
                        last.then_inc(S(f"tp_{kind}"), 1)

        def xt_act(act, kind, u):
            t = STREAM[kind]
            xt_unused(act, kind, u)
            for name, f, j0, nj in xt_names(kind):
                use = Use(kind, u, name)
                use.filled(act)
                act.activation(ln[t]["h"][:, f, j0 * P:(j0 + nj) * P], use.ps[:, 0:nj * P], ACT.Copy)\
                   .then_inc(S(f"xh_{kind}"), 1)

        def xt_dve(dve, kind, u):
            t = STREAM[kind]
            names = xt_names(kind)
            for i, (name, f, j0, nj) in enumerate(names):
                use = Use(kind, u, name)
                dve.wait_ge(S(f"xh_{kind}"), u * len(names) + i + 1)
                dve.tensor_tensor(ln[t]["l"][:, f, j0 * P:(j0 + nj) * P], use.ps[:, 0:nj * P],
                                  ln[t]["h"][:, f, j0 * P:(j0 + nj) * P], ALU.subtract).then_inc(S(use.free), 1)

        def xt_ready(pe, kind, u):
            for name, *_ in xt_names(kind):
                Use(kind, u, name).emptied(pe)

        def wo_pe(pe, kind, u, wh, wl, at):
            for i in range(2):
                use = Use(kind, u, f"W{i}")
                use.claim(pe)
                for jj in range(2):
                    j = 2 * i + jj
                    for k in range(KT):
                        last = mm3(pe, use.ps[:, jj * D:(jj + 1) * D], oh[:, k, j * P:(j + 1) * P],
                                   ol[:, k, j * P:(j + 1) * P], wh[:, at + k * D:at + (k + 1) * D],
                                   wl[:, at + k * D:at + (k + 1) * D], jj == 0 and k == 0, jj == 1 and k == KT - 1)
                last.then_inc(S(use.full), 1)

        def wo_dve(dve, kind, U):
            u, p, q = U
            wait(dve, f"sto{p}", 16 * (q + (NU // 2 if kind == "l1" else 0)))
            for i in range(2):
                use = Use(kind, u, f"W{i}")
                use.filled(dve)
                dve.tensor_tensor(flat(x1[:, p, 2 * i:2 * i + 2, :]), flat(x0[:, p, 2 * i:2 * i + 2, :]),
                                  use.ps[:, :], ALU.add).then_inc(S(use.free), 1)
                use.emptied(dve)
                ln_stats(dve, "ffn" if kind == "l0" else "moe", x1[:, p], (2 * i, 2 * i + 1))

        def x1_ready(eng, kind, u):
            for i in range(2):
                Use(kind, u, f"W{i}").emptied(eng)

        def n0(u, hf, c, g):
            return u * 16 + hf * 8 + c * 2 + g

        def l0_pe(pe, U, s):
            u, p, q = U
            if s == 1:
                xt_pe(pe, "l0", u)
            elif s in (2, 3):
                hf = s - 2
                if s == 2:
                    xt_ready(pe, "l0", u)
                    if isinstance(u, int) and u == 0:
                        pe.wait_ge(S("w_lo"), pieces_to(W1["v"]))
                use = Use("l0", u, f"K{hf}")
                use.claim(pe)
                proj(pe, use.ps[:, :], "a", mh, ml, W1["k"] + hf * P, D, P).then_inc(S(use.full), 1)
                use = Use("l0", u, f"Z{hf}")
                use.claim(pe)
                c = W1["gate"]
                mm3(pe, use.ps[:, :], mh[:, c:c + P], ml[:, c:c + P], ln["a"]["h"][:, hf, :],
                    ln["a"]["l"][:, hf, :], True, True).then_inc(S(use.full), 1)
            elif s in (4, 5):
                hf = s - 4
                use = Use("l0", u, f"R{hf}")
                use.claim(pe)
                Use("l0", u, f"K{hf}").emptied(pe)
                pe.matmul(use.ps[:, :], col("swbd", P), kf[:, hf, :], start=True, stop=True)\
                  .then_inc(S(use.full), 1)
                use = Use("l0", u, f"V{hf}")
                use.claim(pe)
                if isinstance(u, int) and u == 0:
                    pe.wait_ge(S("w_lo"), pieces_to(W1["q"]))
                for i in range(2):
                    j = 2 * hf + i
                    for k in range(KT):
                        c = W1["v"] + k * D
                        last = mm3(pe, use.ps[:, i * D:(i + 1) * D], ln["a"]["h"][:, k, j * P:(j + 1) * P],
                                   ln["a"]["l"][:, k, j * P:(j + 1) * P], mh[:, c:c + D], ml[:, c:c + D],
                                   i == 0 and k == 0, i == 1 and k == KT - 1)
                last.then_inc(S(use.full), 1)
            elif s in (6, 12):
                hf = (s - 6) // 6
                use = Use("l0", u, f"Q{hf}")
                use.claim(pe)
                if isinstance(u, int) and u == 0:
                    pe.wait_ge(S("w_lo"), pieces_to(W1["w1"]))
                proj(pe, use.ps[:, :], "a", mh, ml, W1["q"] + hf * P, D, P).then_inc(S(use.full), 1)
            elif s in (7, 13):
                hf = (s - 7) // 6
                use = Use("l0", u, f"KT{hf}")
                use.claim(pe)
                pe.wait_ge(S("l0_kw"), u * 2 + hf + 1)
                for c in range(NT):
                    last = pe.transpose(use.ps[:, c * P:(c + 1) * P], kf[:, hf, c * P:(c + 1) * P], ident)
                last.then_inc(S(use.full), 1)
            elif s in (8, 14):
                hf = (s - 8) // 6
                use = Use("l0", u, f"dS{hf}")
                use.claim(pe)
                Use("l0", u, f"KT{hf}").emptied(pe)
                for c in range(NT):
                    last = pe.matmul(use.ps[:, c * P:(c + 1) * P], ktok[:, c, :], vtok[:, c, hf * P:(hf + 1) * P],
                                     start=c == 0, stop=c == NT - 1, skip_group_check=True)
                last.then_inc(S(use.full), 1)
                l0_scores(pe, U, hf, 0)
            elif s in (9, 10, 11, 15, 16, 17):
                hf, c = (s - 9) // 6, (s - 9) % 6 + 1
                l0_scores(pe, U, hf, c)
            elif s == 19:
                pe.wait_ge(S("l0_ol"), u * 2 + 2)
                wo_pe(pe, "l0", u, mh, ml, W1["o"])

        def l0_scores(pe, U, hf, c):
            u = U[0]
            for g in range(2):
                use = Use("l0", u, f"A{hf}{c}{g}")
                use.claim(pe)
                if c == 0:
                    pe.wait_ge(S("l0_kl"), u * 2 + hf + 1)
                pe.wait_ge(S("l0_qx"), 2 * n0(u, hf, c, g) + 1)
                kc = slice(c * P, (c + 1) * P)
                pe.matmul(use.ps[:, :], kh[:, kc], qxh[:, g, :], start=True, stop=False)
                pe.matmul(use.ps[:, :], kl[:, kc], qxh[:, g, :], start=False, stop=False)
                pe.wait_ge(S("l0_qx"), 2 * n0(u, hf, c, g) + 2)
                pe.matmul(use.ps[:, :], kh[:, kc], qxl[:, g, :], start=False, stop=True).then_inc(S(use.full), 1)

        def l0_out(pe, U, n):
            u, p, q = U
            hf, c = n // NT, n % NT
            o = accA[:, c * P:(c + 1) * P]
            if c == 0:
                wait(pe, "l0_ol", u * 2 + hf)
                state = st0[:, p, hf, :]
            else:
                pe.wait_ge(S("l0_sx"), u * 6 + hf * 3 + c)
                state = sx[:, c - 1, :]
            pe.matmul(o, state, qp[:, c * P:(c + 1) * P], start=c == 0, stop=False,
                      skip_group_check=True).then_inc(S("l0_inter"), 1)
            for g in range(2):
                m = n0(u, hf, c, g)
                pe.wait_ge(S("l0_vx"), m + 1)
                Use("l0", u, f"A{hf}{c}{g}").emptied(pe)
                for h in range(4):
                    last = pe.matmul(o, vx[:, g, h * P:(h + 1) * P], am[:, (2 * c + g) % 4, h * P:(h + 1) * P],
                                     start=False, stop=c == NT - 1 and g == 1 and h == 3, skip_group_check=True)
                last.then_inc(S("l0_av"), 1)

        def l0_act(act, U, s):
            u, p, q = U
            if s == 0:
                if not (isinstance(u, int) and u <= 1):
                    act.preload_act_table_set("natural_log_exp_and_others")
                ln_act(act, "l0", u)
            elif s == 1:
                xt_act(act, "l0", u)
            elif s in (2, 3):
                hf = s - 2
                m = u * 2 + hf + 1
                use = Use("l0", u, f"K{hf}")
                use.filled(act)
                act.activation(kf[:, hf, :], use.ps[:, :], ACT.Copy).then_inc(S(use.free), 1)
                Use("l0", u, f"Z{hf}").emptied(act)
                act.activation(t1[:, hf, :], t1[:, hf, :], ACT.Exp, scale=-1.0).then_inc(S("l0_ez"), 1)
                act.wait_ge(S("l0_ez"), m)
                act.activation(t1[:, hf, :], t1[:, hf, :], ACT.Ln, bias=1.0).then_inc(S("l0_nlg"), 1)
            elif s in (4, 5):
                hf = s - 4
                m = u * 2 + hf + 1
                use = Use("l0", u, f"R{hf}")
                use.filled(act)
                act.activation(t3[:, hf, :], use.ps[:, :], ACT.Exp, scale=-1.0).then_inc(S("l0_er"), 1)
                use = Use("l0", u, f"V{hf}")
                use.filled(act)
                act.activation(flat(vtok[:, 2 * hf:2 * hf + 2, :]), use.ps[:, :], ACT.Copy)\
                   .then_inc(S(use.free), 1)
                act.wait_ge(S("l0_er"), m)
                act.activation(t3[:, hf, :], t3[:, hf, :], ACT.Ln, bias=1.0).then_inc(S("l0_lr"), 1)
                act.wait_ge(S("l0_clip"), m)
                act.activation(gg[:, hf, :], t1[:, hf, :], ACT.Exp, scale=-1.0).then_inc(S("l0_gc"), 1)
                act.wait_ge(S("l0_gc"), m)
                act.activation(t1[:, hf, :], gg[:, hf, :], ACT.Ln, bias=cst[:, 1:2]).then_inc(S("l0_lg"), 1)
            elif s == 6:
                for hf in range(2):
                    act.wait_ge(S("l0_sum"), u * 2 + hf + 1)
                    act.activation(t3[:, hf, :], t3[:, hf, :], ACT.Exp, scale=-1.0).then_inc(S("l0_ew"), 1)
            if s in (6, 12):
                hf = (s - 6) // 6
                act.wait_ge(S("l0_kw"), u * 2 + hf + 1)
                if hf == 1:
                    Use("l0", u, f"A0{NT - 1}1").filled(act)
                elif not (isinstance(u, int) and u == 0):
                    Use("l0", u - 1, "W1").filled(act)
                act.activation(kh, kf[:, hf, :], ACT.Copy).then_inc(S("l0_kh"), 1)
                Use("l0", u, f"Q{hf}").emptied(act)
                act.activation(qh[:, :], qp[:, :], ACT.Copy).then_inc(S("l0_qh"), 1)
            if s in (13, 18):
                hf = 0 if s == 13 else 1
                act.wait_ge(S("l0_av"), n0(u, hf, NT - 1, 1) + 1)
                if not (isinstance(u, int) and u == 0):
                    Use("l0", u - 1, "W1").filled(act)
                act.activation(oh[:, hf, :], accA[:, :], ACT.Copy).then_inc(S("l0_oh"), 1)

        def l0_dve(dve, U, s):
            u, p, q = U
            if s == 0:
                dve.wait_ge(S(f"ld{p}"), 16 * (q + 1))
                ln_stats(dve, "l0", x0[:, p], range(NT))
                ln_dve(dve, "l0", u)
            elif s == 1:
                norm_dve(dve, "l0", U, (2, 3))
                xt_dve(dve, "l0", u)
            elif s in (2, 3):
                hf = s - 2
                use = Use("l0", u, f"Z{hf}")
                use.filled(dve)
                dve.tensor_scalar(t1[:, hf, :], use.ps[:, :], LOG_GCLIP, None, ALU.max).then_inc(S(use.free), 1)
            elif s in (4, 5):
                hf = s - 4
                m = u * 2 + hf + 1
                dve.wait_ge(S("l0_nlg"), m)
                dve.tensor_tensor_scan(t1[:, hf, :], t1[:, hf, :], zeros[:, 0:1].to_broadcast([P, UT]),
                                       cum[:, p, hf:hf + 1], ALU.add, ALU.add).then_inc(S("l0_cum"), 1)
                use = Use("l0", u, f"R{hf}")
                use.filled(dve)
                dve.wait_ge(S("l0_er"), m)
                dve.tensor_tensor(kf[:, hf, :], kf[:, hf, :], use.ps[:, :], ALU.mult).then_inc(S(use.free), 1)
                dve.wait_ge(S("l0_cum"), m)
                dve.tensor_copy(cum[:, p, hf:hf + 1], t1[:, hf, UT - 1:UT]).then_inc(S("l0_car"), 1)
                dve.wait_ge(S("l0_car"), m)
                dve.tensor_scalar(t1[:, hf, :], t1[:, hf, :], 30.0, -30.0, ALU.min, ALU.max)\
                   .then_inc(S("l0_clip"), 1)
            elif s in (6, 12):
                hf = (s - 6) // 6
                m = u * 2 + hf + 1
                if hf == 0:
                    for h in range(2):
                        dve.wait_ge(S("l0_lg"), m + h)
                        dve.tensor_tensor(t3[:, h, :], t3[:, h, :], t1[:, h, :], ALU.add).then_inc(S("l0_sum"), 1)
                    for h in range(2):
                        dve.wait_ge(S("l0_ew"), m + h)
                        dve.tensor_tensor(kf[:, h, :], kf[:, h, :], t3[:, h, :], ALU.mult).then_inc(S("l0_kw"), 1)
                use = Use("l0", u, f"Q{hf}")
                use.filled(dve)
                wait(dve, "l0_inter", u * 8 + hf * 4)
                dve.wait_ge(S("l0_gc"), m)
                dve.scalar_tensor_tensor(out=qp[:, :], in0=gg[:, hf, :], scalar=GCLIP, in1=use.ps[:, :],
                                         op0=ALU.add, op1=ALU.mult).then_inc(S(use.free), 1)
                dve.wait_ge(S("l0_kh"), m)
                dve.tensor_tensor(kl, kf[:, hf, :], kh, ALU.subtract).then_inc(S("l0_kl"), 1)
                dve.wait_ge(S("l0_qh"), m)
                dve.tensor_tensor(ql[:, :], qp[:, :], qh[:, :], ALU.subtract).then_inc(S("l0_ql"), 1)
            elif s in (7, 13):
                hf = (s - 7) // 6
                use = Use("l0", u, f"KT{hf}")
                use.filled(dve)
                dve.tensor_copy(flat(ktok[:, :, :]), use.ps[:, :]).then_inc(S(use.free), 1)
                if hf == 1:
                    l0_low(dve, U, 0)
            elif s in (8, 14):
                hf = (s - 8) // 6
                m = u * 6 + hf * 3
                use = Use("l0", u, f"dS{hf}")
                use.filled(dve)
                wait(dve, "l0_inter", u * 8 + hf * 4)
                dve.tensor_tensor(dst[:, :].rearrange("p (c e) -> p c e", c=NT),
                                  use.ps[:, :].rearrange("p (c e) -> p c e", c=NT),
                                  bc(col("bd16", P), 1, [P, NT, P]), ALU.mult).then_inc(S(use.free), 1)
                use.emptied(dve)
                dve.tensor_tensor(sx[:, 0, :], st0[:, p, hf, :], dst[:, 0:P], ALU.add).then_inc(S("l0_sx"), 1)
                for c in range(1, NT - 1):
                    dve.wait_ge(S("l0_sx"), m + c)
                    dve.tensor_tensor(sx[:, c, :], sx[:, c - 1, :], dst[:, c * P:(c + 1) * P], ALU.add)\
                       .then_inc(S("l0_sx"), 1)
                l0_mask(dve, U, hf, 0)
            elif s in (9, 10, 11, 15, 16, 17):
                hf, c = (s - 9) // 6, (s - 9) % 6 + 1
                l0_mask(dve, U, hf, c)
                if c == 2:
                    dve.wait_ge(S("l0_inter"), u * 8 + hf * 4 + 1)
                    dve.wait_ge(S("l0_sx"), u * 6 + hf * 3 + 3)
                    dve.tensor_tensor(st0[:, p, hf, :], sx[:, NT - 2, :], dst[:, (NT - 1) * P:NT * P], ALU.add)\
                       .then_inc(S("l0_st"), 1)
            elif s == 18:
                l0_low(dve, U, 1)
            elif s == 19:
                wo_dve(dve, "l0", U)

        def l0_mask(dve, U, hf, c):
            u = U[0]
            for g in range(2):
                use = Use("l0", u, f"A{hf}{c}{g}")
                use.filled(dve)
                wait(dve, "l0_av", n0(u, hf, c, g) - 3)
                dve.tensor_tensor(am[:, (2 * c + g) % 4, :].rearrange("p (h t) -> p h t", h=4),
                                  use.ps[:, :].rearrange("p (h t) -> p h t", h=4),
                                  bc(causal, 1, [P, 4, P]), ALU.mult).then_inc(S(use.free), 1)

        def l0_low(dve, U, hf):
            dve.wait_ge(S("l0_oh"), U[0] * 2 + hf + 1)
            dve.tensor_tensor(ol[:, hf, :], accA[:, :], oh[:, hf, :], ALU.subtract).then_inc(S("l0_ol"), 1)

        def l0_pool(pool, U, s):
            u, p, q = U
            if s < 7 or s == 12 or s > 17:
                return
            hf, c = (s - 7) // 6, (s - 7) % 6
            if c < NT:
                for g in range(2):
                    pool.wait_ge(S("l0_qh"), u * 2 + hf + 1)
                    if c > 0:
                        Use("l0", u, f"A{hf}{c - 1}{g}").filled(pool)
                    elif not (isinstance(u, int) and u == 0 and hf == 0):
                        Use("l0", u - 1 if hf == 0 else u, f"A{1 - hf}{NT - 1}{g}").filled(pool)
                    for part, full in ((qxh, qh), (qxl, ql)):
                        if full is ql and c == 0:
                            pool.wait_ge(S("l0_ql"), u * 2 + hf + 1)
                        pool.tensor_tensor(heads(part[:, g, :]), bc(full[:, c * P:(c + 1) * P], 1, [P, 4, P]),
                                           bc(col("hm16", HH)[:, 4 * g:4 * g + 4], 2, [P, 4, P]), ALU.mult)\
                            .then_inc(S("l0_qx"), 1)
            if c > 0:
                for g in range(2):
                    Use("l0", u, f"V{(c - 1) // 2}").emptied(pool)
                    wait(pool, "l0_av", n0(u, hf, c - 1, g) - 1)
                    d = vx[:, g, g * 64:g * 64 + VX].rearrange("p (h x) -> p h x", x=P + D0)[:, :, 0:D0]
                    at_ = hf * P + g * 64
                    v = vtok[:, c - 1, at_:at_ + 64].rearrange("p (h e) -> p h e", e=D0)
                    pool.tensor_tensor(d, v, bc(zeros[:, 0:1], 2, [P, 4, D0]), ALU.add).then_inc(S("l0_vx"), 1)

        def ffn_pe(pe, U, s):
            u, p, q = U
            if s == 1:
                xt_pe(pe, "ffn", u)
            elif s >= 2:
                j = s - 2
                if j == 0:
                    xt_ready(pe, "ffn", u)
                    if isinstance(u, int) and u == 0:
                        pe.wait_ge(S("w_lo"), M1_PIECES)
                if j < NF:
                    use = Use("ffn", u, f"h{j}")
                    use.claim(pe)
                    proj(pe, use.ps[:, :], "b", mh, ml, W1["w1"] + j * P, F1, P).then_inc(S(use.full), 1)

        def ffn_down(pe, U, i):
            pe.wait_ge(S("ffn_hl"), at("ffn_hl", U[0] * NF + i + 1))
            down_pe(pe, "ffn", U[0], i, NF, W1["w2"] + i * D, "ffn_dn")

        def down_pe(pe, kind, u, i, n, at, done):
            if i == 0:
                wait(pe, "accB_free", seq(kind, u) * 2)
            for j in range(NT):
                last = mm3(pe, accB[j // 2][:, (j % 2) * D:(j % 2 + 1) * D], hh[:, i % 2, j * P:(j + 1) * P],
                           hl[:, i % 2, j * P:(j + 1) * P], mh[:, at:at + D], ml[:, at:at + D],
                           i == 0 and j % 2 == 0, i == n - 1 and j % 2 == 1)
            last.then_inc(S(done), 1)

        def ffn_act(act, U, s):
            u, p, q = U
            if s == 0:
                ln_act(act, "ffn", u)
            elif s == 1:
                xt_act(act, "ffn", u)
            elif s - 2 < NF:
                j = s - 2
                use = Use("ffn", u, f"h{j}")
                use.filled(act)
                wait(act, "ffn_hl", u * NF + max(j - 1, 0))
                act.activation(hfull[:, j % 2, :], use.ps[:, :], ACT.Gelu, bias=col("b1", NF)[:, j:j + 1])\
                   .then_inc(S(use.free), 1)

        def ffn_dve(dve, U, s):
            u, p, q = U
            if s == 0:
                ln_dve(dve, "ffn", u)
            elif s == 1:
                norm_dve(dve, "ffn", U, (2, 3))
                xt_dve(dve, "ffn", u)
            elif s - 2 < NF:
                j = s - 2
                Use("ffn", u, f"h{j}").emptied(dve)
                wait(dve, "ffn_dn", u * NF + max(j - 1, 0))
                dve.tensor_copy(hh[:, j % 2, :], hfull[:, j % 2, :]).then_inc(S("ffn_hh"), 1)
                dve.wait_ge(S("ffn_hh"), u * NF + j + 1)
                dve.tensor_tensor(hl[:, j % 2, :], hfull[:, j % 2, :], hh[:, j % 2, :], ALU.subtract)\
                   .then_inc(S("ffn_hl"), 1)
            elif s == 11:
                dve.wait_ge(S("ffn_xb"), u + 1)
                dve.wait_ge(S("ffn_dn"), at("ffn_dn", u * NF + NF))
                resid_dve(dve, U)

        def resid_dve(dve, U):
            p = U[1]
            for i in range(2):
                x = flat(x1[:, p, 2 * i:2 * i + 2, :])
                dve.tensor_tensor(x, x, accB[i][:, :], ALU.add).then_inc(S("accB_free"), 1)

        def ffn_pool(pool, U, s):
            u, p, q = U
            if s == 1:
                pool.wait_ge(S("xn_b"), seq("ffn", u) * NT + NT)
                pool.tensor_tensor(x1[:, p, :, :], x1[:, p, :, :], bc(col("b2", D), 1, [P, NT, D]), ALU.add)\
                    .then_inc(S("ffn_xb"), 1)

        def l1_pe(pe, U, s):
            u, p, q = U
            if s == 1:
                xt_pe(pe, "l1", u)
            elif s == 2:
                xt_ready(pe, "l1", u)
                if isinstance(u, int) and u == 0:
                    pe.wait_ge(S("w_lo"), M2_AT)
                use = Use("l1", u, "zg")
                use.claim(pe)
                proj(pe, use.ps[:, :], "a", gh, gl, GK, P, P).then_inc(S(use.full), 1)
                l1_vg(pe, U, 0)
            elif s in (3, 4, 5):
                l1_vg(pe, U, s - 2)
            elif s == 6:
                for name in "qk":
                    use = Use("l1", u, name)
                    use.claim(pe)
                    proj(pe, use.ps[:, :], "a", gh, gl, WG[name], P, P).then_inc(S(use.full), 1)
            elif s == 7:
                use = Use("l1", u, "KT")
                use.claim(pe)
                Use("l1", u, "k").emptied(pe)
                for c in range(NT):
                    last = pe.transpose(use.ps[:, c * P:(c + 1) * P], kf[:, 0, c * P:(c + 1) * P], ident)
                last.then_inc(S(use.full), 1)
            elif 8 <= s <= 12:
                c = s - 8
                if c in (1, 2):
                    use = Use("l1", u, f"dS{c - 1}")
                    use.claim(pe)
                    for i in range(2):
                        cc = 2 * (c - 1) + i
                        last = pe.matmul(use.ps[:, i * D:(i + 1) * D], ktok[:, cc, :], vtok[:, cc, :],
                                         start=i == 0, stop=i == 1, skip_group_check=True)
                    last.then_inc(S(use.full), 1)
                if c < NT:
                    use = Use("l1", u, f"A{c}")
                    use.claim(pe)
                    pe.wait_ge(S("l1_qx"), u * NT + c + 1)
                    pe.matmul(use.ps[:, :], kf[:, 0, c * P:(c + 1) * P], qx1[:, c % 2, :], start=True,
                              stop=True).then_inc(S(use.full), 1)
            elif s == 13:
                for f in range(KT):
                    use = Use("l1", u, f"oT{f}")
                    use.claim(pe)
                    pe.wait_ge(S("l1_on"), u * 2 + 2)
                    for c in range(NT):
                        last = pe.transpose(use.ps[:, c * P:(c + 1) * P], on1[:, c, f * P:(f + 1) * P], ident)
                    last.then_inc(S(use.full), 1)
            elif s == 14:
                for f in range(KT):
                    Use("l1", u, f"oT{f}").emptied(pe)
                wo_pe(pe, "l1", u, gh, gl, WG["o"])

        def l1_vg(pe, U, c):
            use = Use("l1", U[0], f"vg{c}")
            use.claim(pe)
            for k in range(KT):
                w = WG["vg"] + k * 512
                last = mm3(pe, use.ps[:, :], ln["a"]["h"][:, k, c * P:(c + 1) * P],
                           ln["a"]["l"][:, k, c * P:(c + 1) * P], gh[:, w:w + 512], gl[:, w:w + 512],
                           k == 0, k == KT - 1)
            last.then_inc(S(use.full), 1)

        def l1_out(pe, U, c):
            u = U[0]
            if c % 2 == 0:
                wait(pe, "l1_acc", u * 2 + c // 2)
            o = accA[:, (c % 2) * D:(c % 2 + 1) * D]
            pe.wait_ge(S("l1_st"), u * 8 + 2 * c + 1)
            pe.matmul(o, qp[:, c * P:(c + 1) * P], sd[:, c, :], start=c % 2 == 0, stop=False,
                      skip_group_check=True)
            Use("l1", u, f"A{c}").emptied(pe)
            for h in range(H1):
                last = pe.matmul(o[:, h * DV:(h + 1) * DV], am[:, c, h * P:(h + 1) * P],
                                 vtok[:, c, h * DV:(h + 1) * DV], start=False, stop=c % 2 == 1 and h == H1 - 1,
                                 skip_group_check=True)
            last.then_inc(S("l1_o"), 1)

        def l1_act(act, U, s):
            u, p, q = U
            if s == 0:
                ln_act(act, "l1", u)
            elif s == 1:
                xt_act(act, "l1", u)
            elif s == 2:
                use = Use("l1", u, "zg")
                use.filled(act)
                act.activation(t1[:, 0, :], use.ps[:, :], ACT.Abs, bias=col("gkb", 1)).then_inc(S("l1_ab"), 1)
                act.activation(t2[:, 0, :], use.ps[:, :], ACT.Relu, bias=ngkb[:, 0:1], scale=-1.0)\
                   .then_inc(S(use.free), 1)
                act.wait_ge(S("l1_ab"), u + 1)
                act.activation(t1[:, 0, :], t1[:, 0, :], ACT.Exp, scale=-1.0).then_inc(S("l1_ea"), 1)
                act.wait_ge(S("l1_ea"), u + 1)
                act.activation(t1[:, 0, :], t1[:, 0, :], ACT.Ln, bias=1.0).then_inc(S("l1_la"), 1)
                l1_gate_act(act, U, 0)
            elif s == 3:
                l1_gate_act(act, U, 1)
            elif s == 4:
                act.wait_ge(S("l1_dm"), u + 1)
                act.activation(dec[:, :], dmid[:, :], ACT.Exp, scale=1.0 / GATE_NORM).then_inc(S("l1_dec"), 1)
                act.wait_ge(S("l1_ex"), u + 1)
                act.activation(t1[:, 0, :], t2[:, 0, :], ACT.Exp, scale=-1.0 / GATE_NORM).then_inc(S("l1_eq"), 1)
                act.activation(t3[:, 0, :], t2[:, 0, :], ACT.Exp, scale=1.0 / GATE_NORM).then_inc(S("l1_ek"), 1)
                l1_gate_act(act, U, 2)
            elif s == 5:
                l1_gate_act(act, U, 3)
            elif s in (10, 12):
                if s == 10 and isinstance(u, int) and u == 0:
                    act.preload_act_table_set("natural_log_exp_and_others")
                i = (s - 10) // 2
                m = u * 2 + i + 1
                act.wait_ge(S("l1_o"), u * NT + 2 * i + 2)
                act.activation(kf[:, 1, :], accA[:, :], ACT.Square).then_inc(S("l1_sq"), 1)
                act.wait_ge(S("l1_ss"), m)
                act.activation(rr[:, i, :], ss[:, i, :], ACT.Ln, scale=1.0 / DV, bias=cst[:, 0:1])\
                   .then_inc(S("l1_ls"), 1)
                act.wait_ge(S("l1_ls"), m)
                act.activation(rr[:, i, :], rr[:, i, :], ACT.Exp, scale=-0.5).then_inc(S("l1_rr"), 1)
            elif s == 13:
                if isinstance(u, int) and u == 0:
                    Use("l0", NU - 1, "W1").filled(act)
                else:
                    Use("l1", u - 1, "W1").filled(act)
                for f in range(KT):
                    use = Use("l1", u, f"oT{f}")
                    use.filled(act)
                    act.activation(oh[:, f, :], use.ps[:, :], ACT.Copy).then_inc(S("l1_oh"), 1)

        def l1_gate_act(act, U, c):
            u = U[0]
            m = u * NT + c + 1
            use = Use("l1", u, f"vg{c}")
            use.filled(act)
            act.activation(vtok[:, c, :], use.ps[:, 0:D], ACT.Copy).then_inc(S("l1_v"), 1)
            act.activation(gate1[:, c, :], use.ps[:, D:2 * D], ACT.Exp, scale=-1.0).then_inc(S("l1_g1"), 1)
            act.wait_ge(S("l1_g1"), m)
            act.activation(gate1[:, c, :], gate1[:, c, :], ACT.Ln, bias=1.0).then_inc(S("l1_g2"), 1)
            act.wait_ge(S("l1_g2"), m)
            act.activation(gate1[:, c, :], gate1[:, c, :], ACT.Exp, scale=-1.0).then_inc(S("l1_g3"), 1)

        def l1_gate_dve(dve, U, c):
            u = U[0]
            use = Use("l1", u, f"vg{c}")
            dve.wait_ge(S("l1_g3"), u * NT + c + 1)
            dve.tensor_tensor(gate1[:, c, :], gate1[:, c, :], use.ps[:, D:2 * D], ALU.mult)\
               .then_inc(S(use.free), 1)

        def l1_dve(dve, U, s):
            u, p, q = U
            if s == 0:
                dve.wait_ge(S(f"ld{p}"), 16 * (q + 1 + NU // 2))
                ln_stats(dve, "l1", x0[:, p], range(NT))
                ln_dve(dve, "l1", u)
            elif s == 1:
                norm_dve(dve, "l1", U, (2, 3))
                xt_dve(dve, "l1", u)
            elif s == 2:
                l1_gate_dve(dve, U, 0)
            elif s == 3:
                dve.wait_ge(S("l1_la"), u + 1)
                Use("l1", u, "zg").emptied(dve)
                dve.tensor_tensor(t1[:, 0, :], t1[:, 0, :], t2[:, 0, :], ALU.add).then_inc(S("l1_nl"), 1)
                dve.wait_ge(S("l1_nl"), u + 1)
                dve.tensor_tensor_scan(t1[:, 0, :], t1[:, 0, :], zeros[:, 0:1].to_broadcast([P, UT]), 0.0,
                                       ALU.add, ALU.add).then_inc(S("l1_cum"), 1)
                dve.wait_ge(S("l1_cum"), u + 1)
                dve.tensor_copy(mid[:, p, 1:NT + 1], t1[:, 0, :].rearrange("p (c t) -> p c t", c=NT)[:, :, P // 2 - 1])\
                   .then_inc(S("l1_mid"), 1)
                dve.wait_ge(S("l1_mid"), u * 2 + 1)
                dve.tensor_tensor(dmid[:, :], mid[:, p, 0:NT], mid[:, p, 1:NT + 1], ALU.subtract)\
                   .then_inc(S("l1_dm"), 1)
                dve.tensor_tensor(t2[:, 0, :].rearrange("p (c t) -> p c t", c=NT),
                                  t1[:, 0, :].rearrange("p (c t) -> p c t", c=NT),
                                  bc(mid[:, p, 1:NT + 1], 2, [P, NT, P]), ALU.subtract).then_inc(S("l1_rel"), 1)
                dve.wait_ge(S("l1_dm"), u + 1)
                dve.tensor_tensor(mid[:, p, 0:1], mid[:, p, NT:NT + 1], t1[:, 0, UT - 1:UT], ALU.subtract)\
                   .then_inc(S("l1_mid"), 1)
                dve.wait_ge(S("l1_rel"), u + 1)
                dve.tensor_scalar(t2[:, 0, :], t2[:, 0, :], SPREAD * GATE_NORM, -SPREAD * GATE_NORM, ALU.min,
                                  ALU.max).then_inc(S("l1_ex"), 1)
                l1_gate_dve(dve, U, 1)
            elif s in (4, 5):
                l1_gate_dve(dve, U, s - 2)
            elif s == 6:
                use = Use("l1", u, "q")
                use.filled(dve)
                dve.wait_ge(S("l1_eq"), u + 1)
                dve.scalar_tensor_tensor(out=qp[:, :], in0=use.ps[:, :], scalar=DK ** -0.5, in1=t1[:, 0, :],
                                         op0=ALU.mult, op1=ALU.mult).then_inc(S(use.free), 1)
                use = Use("l1", u, "k")
                use.filled(dve)
                dve.wait_ge(S("l1_ek"), u + 1)
                dve.tensor_tensor(kf[:, 0, :], use.ps[:, :], t3[:, 0, :], ALU.mult).then_inc(S(use.free), 1)
            elif s == 7:
                use = Use("l1", u, "KT")
                use.filled(dve)
                dve.tensor_copy(flat(ktok[:, :, :]), use.ps[:, :]).then_inc(S(use.free), 1)
                dve.wait_ge(S("l1_dec"), u + 1)
                wait(dve, "l1_st", u * 8)
                l1_decay(dve, U, 0)
            elif 8 <= s <= 12:
                c = s - 8
                if c in (1, 2):
                    use = Use("l1", u, f"dS{c - 1}")
                    use.filled(dve)
                    wait(dve, "l1_st", u * 8 + 1 if c == 1 else u * 8 + 5)
                    dve.tensor_tensor(dst[:, :].rearrange("p (c e) -> p c e", c=2),
                                      use.ps[:, :].rearrange("p (c e) -> p c e", c=2),
                                      bc(col("bd32", D), 1, [P, 2, D]), ALU.mult).then_inc(S(use.free), 1)
                    use.emptied(dve)
                    for i in range(2):
                        cc = 2 * (c - 1) + i
                        m = u * 8 + 2 * cc + 1
                        dve.wait_ge(S("l1_st"), m)
                        dve.tensor_tensor(st1[:, p, :], sd[:, cc, :], dst[:, i * D:(i + 1) * D], ALU.add)\
                           .then_inc(S("l1_st"), 1)
                        if cc < NT - 1:
                            dve.wait_ge(S("l1_st"), m + 1)
                            l1_decay(dve, U, cc + 1)
                if c < NT:
                    use = Use("l1", u, f"A{c}")
                    use.filled(dve)
                    dve.tensor_tensor(am[:, c, :].rearrange("p (h t) -> p h t", h=4),
                                      use.ps[:, :].rearrange("p (h t) -> p h t", h=4),
                                      bc(causal, 1, [P, 4, P]), ALU.mult).then_inc(S(use.free), 1)
                if c in (2, 4):
                    i = c // 2 - 1
                    m = u * 2 + i + 1
                    dve.wait_ge(S("l1_sq"), m)
                    dve.tensor_reduce(ss[:, i, :], kf[:, 1, :].rearrange("p (g v) -> p g v", v=DV),
                                      axis=AX.X, op=ALU.add).then_inc(S("l1_ss"), 1)
                    dve.wait_ge(S("l1_rr"), m)
                    dve.tensor_tensor(t3[:, i, :].rearrange("p (g v) -> p g v", v=DV),
                                      accA[:, :].rearrange("p (g v) -> p g v", v=DV),
                                      bc(rr[:, i, :], 2, [P, 2 * H1, DV]), ALU.mult).then_inc(S("l1_acc"), 1)
            elif s == 13:
                for f in range(KT):
                    use = Use("l1", u, f"oT{f}")
                    dve.wait_ge(S("l1_oh"), u * 2 + f + 1)
                    dve.tensor_tensor(ol[:, f, :], use.ps[:, :], oh[:, f, :], ALU.subtract)\
                       .then_inc(S(use.free), 1)
            elif s == 14:
                wo_dve(dve, "l1", U)

        def l1_decay(dve, U, c):
            dve.tensor_scalar(sd[:, c, :], st1[:, U[1], :], dec[:, c:c + 1], None, ALU.mult)\
               .then_inc(S("l1_st"), 1)

        def l1_pool(pool, U, s):
            u, p, q = U
            if 2 <= s <= 5:
                c = s - 2
                Use("l1", u, f"vg{c}").emptied(pool)
                g = gate1[:, c, :].rearrange("p (h v) -> p h v", v=DV)
                pool.tensor_tensor(g, g, bc(col("gnw", DV), 1, [P, H1, DV]), ALU.mult).then_inc(S("l1_gw"), 1)
            elif 7 <= s <= 10:
                c = s - 7
                Use("l1", u, "q").emptied(pool)
                if c < 2:
                    if isinstance(u, int) and u == 0:
                        Use("l0", NU - 1, "W1").filled(pool)
                    else:
                        Use("l1", u - 1, f"A{c + 2}").filled(pool)
                else:
                    Use("l1", u, f"A{c - 2}").filled(pool)
                pool.tensor_tensor(heads(qx1[:, c % 2, :]), bc(qp[:, c * P:(c + 1) * P], 1, [P, 4, P]),
                                   bc(col("hm32", H1), 2, [P, 4, P]), ALU.mult).then_inc(S("l1_qx"), 1)
                if c == 3:
                    l1_gated(pool, U, 0)
            elif s == 12:
                l1_gated(pool, U, 1)

        def l1_gated(pool, U, i):
            u = U[0]
            pool.wait_ge(S("l1_acc"), u * 2 + 1 + i)
            pool.wait_ge(S("l1_gw"), u * NT + 2 * i + 2)
            pool.tensor_tensor(t3[:, i, :], t3[:, i, :], gg[:, i, :], ALU.mult).then_inc(S("l1_on"), 1)

        def moe_pe(pe, U, s):
            u, p, q = U
            first = isinstance(u, int) and u == 0
            if s == 1:
                xt_pe(pe, "moe", u)
            elif s == 2:
                xt_ready(pe, "moe", u)
                if first:
                    pe.wait_ge(S("w_lo"), M2_AT + 1)
                use = Use("moe", u, "rt")
                use.claim(pe)
                for j in range(NT):
                    for k in range(KT):
                        c = W2["router"] + k * NE
                        last = mm3(pe, use.ps[:, j * NE:(j + 1) * NE], ln["b"]["h"][:, k, j * P:(j + 1) * P],
                                   ln["b"]["l"][:, k, j * P:(j + 1) * P], mh[:, c:c + NE], ml[:, c:c + NE],
                                   j == 0 and k == 0, j == NT - 1 and k == KT - 1)
                last.then_inc(S(use.full), 1)
            elif 3 <= s <= 14:
                e = max(s - 4, 0)
                if s == 4:
                    use = Use("moe", u, "cT")
                    use.claim(pe)
                    pe.wait_ge(S("moe_cw"), u + 1)
                    for j in range(NT):
                        last = pe.transpose(use.ps[0:2 * NE, j * P:(j + 1) * P], cwr[:, j, :].bitcast(f32), ident)
                    last.then_inc(S(use.full), 1)
                elif e <= NE:
                    if first:
                        end = W2[f"wd{e}"] + D
                        pe.wait_ge(S("w_lo"), M2_AT + (end + PIECE - 1) // PIECE)
                    for n in "gu":
                        use = Use("moe", u, f"{n}{e}")
                        use.claim(pe)
                        proj(pe, use.ps[:, :], "b", mh, ml, W2[f"w{n}{e}"], IE, IE).then_inc(S(use.full), 1)
                if 4 <= s < 4 + NE:
                    use = Use("moe", u, f"c{e}")
                    use.claim(pe)
                    Use("moe", u, "cT").emptied(pe)
                    pe.matmul(use.ps[:, :], selr[:, e:e + 1].to_broadcast([2 * NE, P]), cT[:, :], start=True,
                              stop=True).then_inc(S(use.full), 1)

        def moe_down(pe, U, e):
            pe.wait_ge(S("moe_hl"), U[0] * (NE + 1) + e + 1)
            down_pe(pe, "moe", U[0], e, NE + 1, W2[f"wd{e}"], "moe_dn")

        def moe_act(act, U, s):
            u, p, q = U
            if s == 0:
                ln_act(act, "moe", u)
            elif s == 1:
                xt_act(act, "moe", u)
            elif s == 2:
                use = Use("moe", u, "rt")
                use.filled(act)
                act.activation(flat(sc[:, :, :]), use.ps[:, 0:NT * NE], ACT.Exp, scale=-1.0)\
                   .then_inc(S(use.free), 1)
            elif s == 3 or 5 <= s <= 13:
                e = 0 if s == 3 else s - 4
                n = u * (NE + 1) + e
                if e >= 1:
                    moe_h_ready(act, u, e - 1)
                    wait(act, "moe_dn", n - min(e, 2))
                    act.activation(hh[:, (e - 1) % 2, :], hfull[:, (e - 1) % 2, :], ACT.Copy)\
                       .then_inc(S("moe_hh"), 1)
                if e <= NE:
                    use = Use("moe", u, f"g{e}")
                    use.filled(act)
                    act.activation(sg[:, e % 2, :], use.ps[:, :], ACT.Exp, scale=-1.0).then_inc(S("moe_e1"), 1)
                    act.wait_ge(S("moe_e1"), n + 1)
                    act.activation(sg[:, e % 2, :], sg[:, e % 2, :], ACT.Ln, bias=1.0).then_inc(S("moe_e2"), 1)
                    act.wait_ge(S("moe_e2"), n + 1)
                    act.activation(sg[:, e % 2, :], sg[:, e % 2, :], ACT.Exp, scale=-1.0)\
                       .then_inc(S("moe_sg"), 1)

        ROUTE = 16

        def route_dve(dve, u):
            k = [0]

            def link(ins):
                k[0] += 1
                ins.then_inc(S("moe_rt"), 1)
                dve.wait_ge(S("moe_rt"), u * ROUTE + k[0])

            v4 = sc4[:, :, :].rearrange("p t (g e) -> p (t g) e", g=2)
            scf, sc4f = flat(sc[:, :, :]), flat(sc4[:, :, :])
            link(dve.tensor_scalar(scf, scf, 1.0, None, ALU.add))
            link(dve.reciprocal(scf, scf))
            link(dve.tensor_tensor(sc4[:, :, :], sc[:, :, :], bc(col("cbias", NE), 1, [P, NT, NE]), ALU.add))
            link(dve.tensor_tensor(pr[:, :, 0:3], v4[:, :, 0:3], v4[:, :, 1:4], ALU.add))
            link(dve.tensor_tensor(pr[:, :, 3:5], v4[:, :, 0:2], v4[:, :, 2:4], ALU.add))
            link(dve.tensor_tensor(pr[:, :, 5:6], v4[:, :, 0:1], v4[:, :, 3:4], ALU.add))
            link(dve.tensor_reduce(flat(gs[:, :, :]), pr[:, :, :], axis=AX.X, op=ALU.max))
            link(dve.tensor_tensor(gm[:, :, 0], gs[:, :, 0], gs[:, :, 1], ALU.is_ge))
            link(dve.tensor_tensor(gm[:, :, 1], gs[:, :, 0], gs[:, :, 1], ALU.is_lt))
            link(dve.tensor_tensor(v4, v4, bc(flat(gm[:, :, :]), 2, [P, 2 * NT, NE // 2]), ALU.mult))
            mj = bc(sc4[:, :, :], 2, [P, NT, NE, NE])
            mi = bc(sc4[:, :, :], 3, [P, NT, NE, NE])
            link(dve.tensor_tensor(cmp1[:, :, :, :], mj, mi, ALU.is_gt))
            link(dve.tensor_tensor(cmp2[:, :, :, :], mj, mi, ALU.is_equal))
            c1 = cmp1[:, :, :, :].rearrange("p t i j -> p t (i j)")
            c2 = cmp2[:, :, :, :].rearrange("p t i j -> p t (i j)")
            link(dve.tensor_tensor(c2, c2, bc(col("tri", NE * NE), 1, [P, NT, NE * NE]), ALU.mult))
            link(dve.tensor_tensor(c1, c1, c2, ALU.add))
            link(dve.tensor_reduce(flat(rk[:, :, :]), cmp1[:, :, :, :].rearrange("p t i j -> p (t i) j"),
                                   axis=AX.X, op=ALU.add))
            link(dve.scalar_tensor_tensor(out=flat(cw[:, :, :]), in0=flat(rk[:, :, :]), scalar=1.5, in1=scf,
                                          op0=ALU.is_lt, op1=ALU.mult))
            assert k[0] == ROUTE
            dve.tensor_reduce(dn[:, 0, :], cw[:, :, :], axis=AX.X, op=ALU.add).then_inc(S("moe_ds"), 1)
            dve.wait_ge(S("moe_ds"), u * 2 + 1)
            dve.tensor_scalar(dn[:, 1, :], dn[:, 0, :], 1e-20, None, ALU.add).then_inc(S("moe_ds"), 1)
            dve.wait_ge(S("moe_ds"), u * 2 + 2)
            dve.reciprocal(dn[:, 0, :], dn[:, 1, :]).then_inc(S("moe_rd"), 1)
            dve.wait_ge(S("moe_rd"), u + 1)
            dve.tensor_tensor(cw[:, :, :], cw[:, :, :], bc(dn[:, 0, :], 2, [P, NT, NE]), ALU.mult)\
               .then_inc(S("moe_nw"), 1)
            dve.wait_ge(S("moe_nw"), u + 1)
            dve.tensor_copy(cwr[:, :, 0:NE], cw[:, :, :]).then_inc(S("moe_ch"), 1)
            dve.wait_ge(S("moe_ch"), u + 1)
            dve.tensor_tensor(cwr[:, :, NE:2 * NE], cw[:, :, :], cwr[:, :, 0:NE], ALU.subtract)\
               .then_inc(S("moe_cw"), 1)

        def moe_dve(dve, U, s):
            u, p, q = U
            if s == 0:
                ln_dve(dve, "moe", u)
            elif s == 1:
                norm_dve(dve, "moe", U, (2, 3))
                xt_dve(dve, "moe", u)
            elif s == 2:
                Use("moe", u, "rt").emptied(dve)
                route_dve(dve, u)
            elif 3 <= s <= 12:
                e = max(s - 4, 0)
                n = u * (NE + 1) + e
                h = hfull[:, e % 2, :]
                if s != 4:
                    wait(dve, "moe_hl", n - min(e, 1))
                    if isinstance(u, int) and u == 0 and e < 2:
                        dve.wait_ge(S("ffn_hl"), at("ffn_hl", NU * NF))
                    use = Use("moe", u, f"g{e}")
                    dve.wait_ge(S("moe_sg"), n + 1)
                    dve.tensor_tensor(h, sg[:, e % 2, :], use.ps[:, :], ALU.mult).then_inc(S(use.free), 1)
                    use.emptied(dve)
                    use = Use("moe", u, f"u{e}")
                    use.filled(dve)
                    if e < NE:
                        dve.tensor_tensor(sg[:, e % 2, :], h, use.ps[:, :], ALU.mult).then_inc(S(use.free), 1)
                    else:
                        dve.tensor_tensor(h, h, use.ps[:, :], ALU.mult).then_inc(S(use.free), 1)
                if s == 4:
                    use = Use("moe", u, "cT")
                    use.filled(dve)
                    dve.tensor_copy(cT[:, :], use.ps[0:2 * NE, :]).then_inc(S(use.free), 1)
                if 4 <= s < 4 + NE:
                    Use("moe", u, f"u{e}").emptied(dve)
                    use = Use("moe", u, f"c{e}")
                    use.filled(dve)
                    dve.tensor_tensor(h, sg[:, e % 2, :], use.ps[:, :], ALU.mult).then_inc(S(use.free), 1)
            elif s == 15:
                dve.wait_ge(S("moe_dn"), u * (NE + 1) + NE + 1)
                resid_dve(dve, U)

        def moe_h_ready(eng, u, e):
            Use("moe", u, f"c{e}" if e < NE else f"u{e}").emptied(eng)

        def moe_pool(pool, U, s):
            u, p, q = U
            if 5 <= s <= 13:
                e = s - 5
                n = u * (NE + 1) + e
                pool.wait_ge(S("moe_hh"), n + 1)
                pool.tensor_tensor(hl[:, e % 2, :], hfull[:, e % 2, :], hh[:, e % 2, :], ALU.subtract)\
                    .then_inc(S("moe_hl"), 1)

        ORDER = {
            "l0": {
                "pe": "a2 b0 a3 a4 a5 b1 a6 b2 a7 b3 b4 d0 a8 d1 b5 a9 o0 b6 a10 o1 d2 b7 d3 a11 o2 a12 o3 a13 b8 "
                      "d4 a14 b9 d5 a15 o4 a16 c0 o5 d6 a17 o6 o7 c1 d7 a19",
                "act": "a2 a3 b0 a4 a5 b1 a6 a7 b2 b3 a8 b4 b5 a9 a10 a11 b6 a12 b7 a13 a14 b8 b9 c0 a15 a16 a17 "
                       "a18 b10 c1 b11 a19",
                "dve": "a2 b0 a3 a4 a5 m0 b1 a6 b2 a7 b3 b4 a8 b5 a9 b6 a10 a11 a12 b7 a13 a14 b8 c0 a15 b9 b10 "
                       "a16 a17 n0 c1 a18 b11 a19",
                "pool": "a2 a3 a4 a5 a6 b0 b1 a7 b2 b3 b4 b5 a8 a9 b6 a10 a11 b7 a12 a13 a14 b8 a15 b9 a16 b10 b11 "
                        "a17 c0 a18 c1 a19",
            },
            "l1": {
                "pe": "a2 b0 a3 a4 b1 a5 b2 a6 b3 a7 a8 a9 o0 b4 a10 o1 b5 a11 o2 b6 d0 b7 d1 b8 d2 a12 c0 o3 b9 "
                      "d3 b10 a13 d4 b11 d5 b12 d6 b13 d7 c1 d8 a14",
                "act": "a2 b0 a3 b1 a4 a5 b2 a6 a7 b3 a8 a9 a10 b4 b5 a11 b6 b7 b8 a12 b9 b10 b11 a13 b12 c0 b13 "
                       "b14 b15 a14 c1",
                "dve": "b0 a2 a3 m0 b1 a4 a5 b2 a6 b3 a7 a8 a9 b4 a10 b5 a11 b6 b7 b8 a12 b9 b10 c0 b11 a13 b12 n0 "
                       "c1 b13 b14 b15 a14",
                "pool": "a2 a3 a4 b0 b1 b2 a5 b3 a6 a7 a8 a9 b4 a10 b5 b6 a11 b7 b8 c0 a12 b9 b10 a13 b11 b12 a14 "
                        "b13 b14 c1 b15",
            },
            "turn": {
                "pe": "b0 a0 a1 b1 a2 a3 a4 b2 a5 b3 a6 b4 a7 b5 d0 a8 d1 d2 d3 b6 b7 c0 b8 d4 b9 a9 d5 o0 a10 "
                      "b10 o1 d6 a11 o2 a12 o3 b11 d7 a13 c1 a14",
                "act": "b0 a0 a1 b1 a2 a3 a4 a5 b2 b3 b4 a6 a7 b5 a8 c0 b6 b7 b8 a9 b9 a10 a11 a12 b10 b11 a13 c1 "
                       "a14",
                "dve": "b0 a0 m0 N0 a1 b1 a2 a3 a4 a5 a6 b2 b3 a7 c0 b4 b5 b6 b7 b8 a8 a9 b9 a10 b10 a11 a12 n0 "
                       "b11 a13 c1 a14",
                "pool": "a0 a1 b0 b1 a2 a3 a4 a5 b2 b3 a6 b4 b5 b6 b7 c0 b8 b9 a7 a8 a9 b10 a10 a11 b11 a12 a13 c1 "
                        "a14",
            },
        }

        def beside(eng, a, ua, b, ub, uc, order=None):
            units = {"a": (a, ua), "b": (b, ub), "c": (a, uc), "o": (a + " out", ua), "d": (b + " down", ub),
                     "n": (a + " norm", uc), "m": (b + " norm", ub), "N": (a + " norm", ua)}
            return [(*units[x_[0]], int(x_[1:])) for x_ in ORDER[order or a][eng].split()
                    if units[x_[0]][1] is not None]

        def unit(u):
            return (u, u % 2, u // 2)

        def program(name, eng, fns, prep, edge):
            def run(steps, preps={}):
                for n, (kind, U, s) in enumerate(steps):
                    for i in preps.get(n, ()):
                        prep(i)
                    fns[kind](eng, U, s)

            def rounds(a, b):
                edge(a, "rounds", None)
                with eng.Fori(0, (NU - 2) // 2) as i:
                    for r in range(2):
                        edge(a, "round", (2 * i + r, r, i))
                        run(beside(name, a, (2 * i + r + 1, 1 - r, i + r), b, (2 * i + r, r, i),
                                   (2 * i + r + 2, r, i + 1)))
                        edge(b, "stored", (2 * i + r, r, i))
                edge(a, "last round", None)
                run(beside(name, a, unit(NU - 1), b, unit(NU - 2), None))
                edge(b, "stored", unit(NU - 2))

            edge("l0", "start", None)
            steps = beside(name, "l0", None, "ffn", None, unit(0)) + beside(name, "l0", unit(0), "ffn", None, unit(1))
            run(steps, {steps.index(("l0", unit(0), 2 + i // 2)): [j for j in (i, i + 1) if j < M2_AT]
                        for i in range(0, M2_AT, 2)})
            rounds("l0", "ffn")
            edge("l1", "start", None)
            steps = beside(name, "l1", unit(0), "ffn", unit(NU - 1), unit(1), "turn")
            kinds = [(x_[0], x_[2]) for x_ in steps]
            after_w1, after_w2 = kinds.index(("ffn", 9)) + 1, kinds.index(("ffn", 11)) + 1
            preps = {}
            for at_, first, end in ((kinds.index(("ffn", 1)), 0, FREE_1), (after_w1, FREE_1, FREE_2),
                                    (after_w2, FREE_2, M2_PIECES)):
                for i in range(first, end):
                    preps.setdefault(at_ + (i - first) // 2, []).append(M2_AT + i)
            run(steps, preps)
            edge("ffn", "stored", unit(NU - 1))
            rounds("l1", "moe")
            run(beside(name, "l1", None, "moe", unit(NU - 1), None))
            edge("moe", "stored", unit(NU - 1))

        def pieces_to(c):
            return -(-c // PIECE)

        PIECES = [(wm1, mh, ml, a, n) for a, n in pieces(W1_COLS)] + [(wg, gh, gl, a, n) for a, n in pieces(WG_COLS)]
        M1_PIECES, GK_AT = len(pieces(W1_COLS)), len(PIECES)
        PIECES.append((wgk, gh, gl, 0, GK_RAW))
        M2_AT, M2_PIECES = len(PIECES), len(pieces(W2_COLS))
        PIECES += [(wm2, mh, ml, a, n) for a, n in pieces(W2_COLS)]
        FREE_1, FREE_2 = W1["w1"] // PIECE, W1["w2"] // PIECE
        N_INIT = 8

        def nothing(*_):
            pass

        block = ctx.enter_context(nc.Block())

        @block.sync
        def _(sp):
            def load(src, U):
                u, p, q = U
                sp.dma_start(x0[:, p, :, :], src[bass.ds(u, 1)].rearrange("a p j d -> p (a j) d"))\
                  .then_inc(S(f"ld{p}"), 16)

            def piece(i):
                if i >= 2:
                    sp.wait_ge(S("w_lo"), i - 1)
                src, _, _, a, n = PIECES[i]
                sp.dma_start(stage[:, i % 2, 0:n], src[:, a:a + n]).then_inc(S(f"w_ld{i % 2}"), 16)

            def edge(kind, what, U):
                if what == "start" and kind == "l1":
                    x1_ready(sp, "l0", NU - 1)
                    sp.wait_ge(S("sto1"), at("sto1", 16 * (NU // 2 - 1)))
                    load(scratch, unit(1))
                elif what == "last round" and kind == "l0":
                    x1_ready(sp, "l0", NU - 2)
                    sp.wait_ge(S("sto0"), at("sto0", 16 * (NU // 2 - 1)))
                    load(scratch, unit(0))
                elif what == "rounds" and kind == "l1":
                    for p in range(2):
                        sp.wait_ge(S(f"sto{p}"), at(f"sto{p}", 16 * (NU // 2)))
                elif what == "round":
                    u, p, q = U
                    x1_ready(sp, kind, u)
                    load(x if kind == "l0" else scratch, (u + 2, p, q))
                elif what == "stored":
                    u, p, q = U
                    sp.wait_ge(S("accB_free"), at("accB_free", seq(kind, u) * 2 + 2))
                    dst_ = scratch if kind == "ffn" else out
                    sp.dma_start(dst_[bass.ds(u, 1)].rearrange("a p j d -> p (a j) d"), x1[:, p, :, :])\
                      .then_inc(S(f"sto{p}"), 16)

            load(x, unit(0))
            sp.dma_start(sm[:, :], small).then_inc(S("ld_sm"), 16)
            load(x, unit(1))
            steps = {k: nothing for k in USES}
            program("act", sp, steps, piece, edge)
            for p in range(2):
                sp.wait_ge(S(f"sto{p}"), at(f"sto{p}", 16 * NU))

        @block.gpsimd
        def _(pool):
            for t in (st0, cum, st1, mid, zeros, vx):
                pool.memset(t[tuple(slice(None) for _ in t.shape)], 0.0).then_inc(S("init"), 1)
            pool.memset(cst[:, 0:1], EPS).then_inc(S("init"), 1)
            pool.memset(cst[:, 1:2], GCLIP).then_inc(S("init"), 1)
            for i, name in enumerate(START_AT_ONE):
                pool.memset(cst[:, i + 2:i + 3], 0.0).then_inc(S(name), 1)
            pool.wait_ge(S("init"), N_INIT)
            pool.wait_ge(S("ld_sm"), 16)
            program("pool", pool, {"l0": l0_pool, "ffn": ffn_pool, "l1": l1_pool, "moe": moe_pool}, nothing, nothing)

        @block.scalar
        def _(act):
            act.wait_ge(S("ld_sm"), 16)
            act.wait_ge(S("init"), N_INIT)
            act.activation(ngkb[:, :], col("gkb", 1), ACT.Copy, scale=-1.0).then_inc(S("ngkb"), 1)
            act.wait_ge(S("ngkb"), 1)

            def split_high(i):
                act.wait_ge(S(f"w_ld{i % 2}"), 16 * (i // 2 + 1))
                if i == GK_AT:
                    act.wait_ge(S("gk_full"), 1)
                    act.activation(gh[:, GK:G_COLS], gk_ps, ACT.Copy).then_inc(S("w_hi"), 1)
                    return
                _, hi, lo, a, n = PIECES[i]
                if i == M2_AT:
                    Use("l0", NU - 1, "W1").filled(act)
                elif i == M2_AT + FREE_1:
                    Use("ffn", NU - 1, f"h{NF - 1}").filled(act)
                elif i == M2_AT + FREE_2:
                    act.wait_ge(S("ffn_dn"), at("ffn_dn", NU * NF))
                act.activation(hi[:, a:a + n], stage[:, i % 2, 0:n], ACT.Copy).then_inc(S("w_hi"), 1)

            def edge(kind, what, U):
                if what == "start":
                    act.preload_act_table_set("natural_log_exp_and_others")

            program("act", act, {"l0": l0_act, "ffn": ffn_act, "l1": l1_act, "moe": moe_act}, split_high, edge)

        @block.vector
        def _(dve):
            dve.wait_ge(S("init"), N_INIT)
            dve.wait_ge(S("ld_sm"), 16)
            dve.tensor_copy(selr[:, :], col("sel", NE, 16)).then_inc(S("selr"), 1)

            def split_low(i):
                _, hi, lo, a, n = PIECES[i]
                dve.wait_ge(S("w_hi"), i + 1)
                if i == GK_AT:
                    dve.tensor_tensor(gl[:, GK:G_COLS], gk_ps, gh[:, GK:G_COLS], ALU.subtract)\
                       .then_inc(S("w_lo"), 1)
                    return
                dve.tensor_tensor(lo[:, a:a + n], stage[:, i % 2, 0:n], hi[:, a:a + n], ALU.subtract)\
                   .then_inc(S("w_lo"), 1)

            def first_norm(kind):
                def norm(dve, U, s):
                    norm_dve(dve, kind, U, (0, 1))
                return norm

            fns = {"l0": l0_dve, "ffn": ffn_dve, "l1": l1_dve, "moe": moe_dve}
            fns.update({f"{kind} norm": first_norm(kind) for kind in USES})
            program("dve", dve, fns, split_low, nothing)

        @block.tensor
        def _(pe):
            pe.wait_ge(S("ld_sm"), 16)
            pe.wait_ge(S("selr"), 1)

            def gate_product(i):
                if i != GK_AT:
                    return
                raw = stage[0:GK_RANK, i % 2, :]
                pe.wait_ge(S(f"w_ld{i % 2}"), 16 * (i // 2 + 1))
                for k in range(KT):
                    last = pe.matmul(gk_ps[:, k * P:(k + 1) * P], raw[:, k * P:(k + 1) * P], raw[:, D:D + P],
                                     start=k == 0, stop=k == KT - 1, skip_group_check=True)
                last.then_inc(S("gk_full"), 1)

            program("pe", pe, {"l0": l0_pe, "l0 out": l0_out, "ffn": ffn_pe, "ffn down": ffn_down, "l1": l1_pe,
                              "l1 out": l1_out, "moe": moe_pe, "moe down": moe_down}, gate_product, nothing)


def kernel(**inputs):
    import numpy as np
    import concourse.bacc as bacc
    from concourse.bass_utils import run_bass_kernel_spmd

    a = {k: np.asarray(v) for k, v in inputs.items()}
    f32 = np.float32

    def ktiles(w):
        k, n = w.shape
        return w.reshape(k // P, P, n).transpose(1, 0, 2).reshape(P, -1)

    def pack(cols, at, parts):
        out = np.zeros((P, cols), f32)
        for name, w in parts.items():
            out[0:w.shape[0], at[name]:at[name] + w.shape[1]] = w
        return out

    def block_diag(row):
        out = np.zeros((HH, D0, HH, D0), f32)
        for h in range(HH):
            out[h, :, h, :] = row.reshape(D0, 1)
        return out.reshape(P, P)

    wm1 = pack(W1_COLS, W1, {
        "k": ktiles(a["L0_attn_Wk"].T), "q": ktiles(a["L0_attn_Wq"].T), "v": ktiles(a["L0_attn_Wv"].T),
        "o": ktiles(a["L0_attn_Wo"].T), "gate": block_diag(a["L0_attn_gw"]),
        "w1": ktiles(a["L0_ffn_w1"]), "w2": ktiles(a["L0_ffn_w2"])})
    experts = {"router": ktiles(a["L1_ffn_router_weight"].T)}
    for e in range(NE + 1):
        for n, name in (("wg", "gate"), ("wu", "up"), ("wd", "down")):
            w = a[f"L1_ffn_w_{name}"][e] if e < NE else a[f"L1_ffn_sw_{name}"]
            experts[f"{n}{e}"] = ktiles(w)
    wm2 = pack(W2_COLS, W2, experts)
    vg = np.concatenate([a["L1_attn_Wv"], a["L1_attn_Wg"]], axis=1)
    wg = pack(WG_COLS, WG, {"q": ktiles(a["L1_attn_Wq"]), "k": ktiles(a["L1_attn_Wk"]), "vg": ktiles(vg),
                            "o": ktiles(a["L1_attn_Wo"])})
    wgk = np.zeros((P, GK_RAW), f32)
    wgk[0:GK_RANK, 0:D] = a["L1_attn_gk_w1"].T
    wgk[0:GK_RANK, D:] = a["L1_attn_gk_w2"]
    r = np.arange(P)
    e = np.arange(NE)
    sel = np.zeros((P, NE), f32)
    sel[e, e] = 1
    sel[NE + e, e] = 1
    small = pack(SM_COLS, SM, {
        "swbd": block_diag(a["L0_attn_sw"]), "ident": np.eye(P, dtype=f32),
        "causal": (r[:, None] <= r[None, :]).astype(f32),
        "bd16": (r[:, None] // D0 == r[None, :] // D0).astype(f32),
        "bd32": (r[:, None] // DK == np.arange(D)[None, :] // DV).astype(f32),
        "hm16": (r[:, None] // D0 == np.arange(HH)[None, :]).astype(f32),
        "hm32": (r[:, None] // DK == np.arange(H1)[None, :]).astype(f32),
        "tri": np.broadcast_to((e[:, None] > e[None, :]).astype(f32).reshape(1, -1), (P, NE * NE)),
        "sel": sel, "b1": a["L0_ffn_b1"].reshape(NF, P).T, "gkb": a["L1_attn_gk_b2"].reshape(P, 1),
        "gnw": np.broadcast_to(a["L1_attn_g_norm_w"], (P, DV)), "b2": np.broadcast_to(a["L0_ffn_b2"], (P, D)),
        "cbias": np.broadcast_to(a["L1_ffn_correction_bias"], (P, NE))})
    xs = a["L0_attn_x"].reshape(B, NU // B, NT, P, D).transpose(1, 0, 3, 2, 4).reshape(NU, P, NT, D)

    arrays = {"x": np.ascontiguousarray(xs), "wm1": wm1, "wm2": wm2, "wg": wg, "wgk": wgk, "small": small}
    nc = bacc.Bacc("TRN2", target_bir_lowering=False, num_devices=1)
    dt = mybir.dt.float32
    args = [nc.dram_tensor(f"in_{k}", v.shape, dt, kind="ExternalInput").ap() for k, v in arrays.items()]
    scratch = nc.dram_tensor("between", (NU, P, NT, D), dt, kind="Internal").ap()
    out = nc.dram_tensor("out", (NU, P, NT, D), dt, kind="ExternalOutput").ap()
    build(nc, *args, scratch, out)
    res = run_bass_kernel_spmd(nc, [{f"in_{k}": v for k, v in arrays.items()}], core_ids=[0])
    got = np.asarray(res.results[0]["out"])
    return got.reshape(NU // B, B, P, NT, D).transpose(1, 0, 3, 2, 4).reshape(B, L, D)
```
